# Optimizing a Trainium2 kernel written in Bass

```python
import numpy as np
import jax
import jax.numpy as jnp

def _softmax(x, axis=-1):
    return jax.nn.softmax(x, axis=axis)

def _gelu(x):
    return jax.nn.gelu(x, approximate=True)

def _silu(x):
    return jax.nn.silu(x)

def _sigmoid(x):
    return jax.nn.sigmoid(x)

def _layernorm(x, axis=-1, eps=1e-05):
    m = jnp.mean(x, axis=axis, keepdims=True)
    v = jnp.var(x, axis=axis, keepdims=True)
    return (x - m) / jnp.sqrt(v + eps)

def _scatter_add(tgt, idx, src, axis=0):
    return tgt.at[idx].add(src)

def _segment_sum(src, seg, n):
    return jax.ops.segment_sum(src, seg, n)
kernel_name = 'mk_perceiver_d1_seqx_r4_6a655e'

def setup_inputs(seed: int=0):
    np.random.seed(seed)
    _w = jnp.asarray

    def _rec_inputs():
        import jax
        import jax.numpy as jnp
        _rk = jax.random.key(seed)
        x = 6.313e-05 + 0.9998 * jax.random.normal(jax.random.fold_in(_rk, 1), (32, 64, 256), jnp.float32)
        _lenS = 64 - jax.random.randint(jax.random.fold_in(_rk, 7), (32,), 0, max(1, 64 // 4) + 1, jnp.int32)
        _lenS2 = 1601 - jax.random.randint(jax.random.fold_in(_rk, 8), (32,), 0, max(1, 1601 // 4) + 1, jnp.int32)
        _ctx_1024P = jax.random.normal(jax.random.fold_in(_rk, 11), (32, 16, 256), jnp.float32)
        _ctx_1024c = jax.random.dirichlet(jax.random.fold_in(_rk, 511), 0.3 * jnp.ones((16,), jnp.float32), (32, 1601))
        _ctx_1024t = jnp.einsum('bsk,bkd->bsd', _ctx_1024c, _ctx_1024P)
        _ctx_1024t = _ctx_1024t * jax.lax.rsqrt(jnp.mean(jnp.square(_ctx_1024t)) + 1e-12) * 0.953939
        ctx_1024 = -0.000214406 + 1.00034 * (_ctx_1024t + 0.3 * jax.random.normal(jax.random.fold_in(_rk, 611), (32, 1601, 256), jnp.float32))
        return (x, ctx_1024)
    x, ctx_1024 = _rec_inputs()

    def _L0_xattn_setup():
        import jax, jax.numpy as jnp
        import numpy as np
        from jax import lax
        BIG = jnp.float32(1e+30)

        def _pairwise_euclidean(a, b):
            aa = jnp.sum(a * a, axis=-1)[:, None]
            bb = jnp.sum(b * b, axis=-1)[None, :]
            ab = a @ b.T
            return jnp.sqrt(jnp.maximum(aa + bb - 2.0 * ab, 0.0))

        def _dtw_cost(D):
            row0 = jnp.cumsum(D[0])

            def row_step(prev_row, d_row):
                first = d_row[0] + prev_row[0]

                def col_step(left, inp):
                    d_ij, up, diag = inp
                    r = d_ij + jnp.minimum(jnp.minimum(up, left), diag)
                    return (r, r)
                _, rest = lax.scan(col_step, first, (d_row[1:], prev_row[1:], prev_row[:-1]))
                row = jnp.concatenate([first[None], rest])
                return (row, row)
            _, rows = lax.scan(row_step, row0, D[1:])
            return jnp.concatenate([row0[None], rows], axis=0)

        def _backtrack(R, T1, T2):
            L = T1 + T2 - 1

            def step(carry, _):
                i, j, done = carry
                valid = jnp.logical_not(done)
                cd = jnp.where((i > 0) & (j > 0), R[jnp.maximum(i - 1, 0), jnp.maximum(j - 1, 0)], BIG)
                cu = jnp.where(i > 0, R[jnp.maximum(i - 1, 0), j], BIG)
                cl = jnp.where(j > 0, R[i, jnp.maximum(j - 1, 0)], BIG)
                choice = jnp.argmin(jnp.stack([cd, cu, cl]))
                ni = jnp.where(choice <= 1, i - 1, i)
                nj = jnp.where((choice == 0) | (choice == 2), j - 1, j)
                at_origin = (i == 0) & (j == 0)
                ni = jnp.where(at_origin, 0, ni)
                nj = jnp.where(at_origin, 0, nj)
                return ((ni, nj, done | at_origin), (i, j, valid))
            init = (jnp.int32(T1 - 1), jnp.int32(T2 - 1), jnp.bool_(False))
            _, (i_idx, j_idx, valid) = lax.scan(step, init, None, length=L)
            return (i_idx, j_idx, valid)

        def _align_one(small, large):
            T_small, d = small.shape
            T_large = large.shape[0]
            D = _pairwise_euclidean(small, large)
            R = _dtw_cost(D)
            i_idx, j_idx, valid = _backtrack(R, T_small, T_large)
            contrib = small[i_idx] * valid[:, None].astype(small.dtype)
            expanded = jnp.zeros((T_large, d), dtype=small.dtype).at[j_idx].add(contrib)
            return expanded
        key = jax.random.key(seed)
        k1, k2 = jax.random.split(key)
        teacher = jax.random.normal(k1, (16, 100, 256), dtype=jnp.float32)
        student = jax.random.normal(k2, (16, 150, 256), dtype=jnp.float32)
        return {'teacher_features': teacher, 'student_features': student}
    _L0_xattn_all = _L0_xattn_setup()
    _L0_xattn_in = {k: v for k, v in _L0_xattn_all.items() if k in ()}
    del _L0_xattn_all

    def _L0_attn_setup():
        import jax, jax.numpy as jnp
        import numpy as np
        B, T, D, NH = (4, 512, 256, 16)
        HD = D // NH

        def _rwkv7_forward(x, Wr, Wk, Wv, Ww, Wo):
            b, t, d = x.shape
            nh, hd = (NH, d // NH)
            r = jax.nn.sigmoid(x @ Wr.T).reshape(b, t, nh, hd)
            k = (x @ Wk.T).reshape(b, t, nh, hd)
            v = (x @ Wv.T).reshape(b, t, nh, hd)
            w = (jax.nn.sigmoid(x @ Ww.T) * 0.99).reshape(b, t, nh, hd)

            def step(state, inp):
                w_t, k_t, v_t, r_t = inp
                state = state * w_t[..., :, None] + v_t[..., :, None] * k_t[..., None, :]
                out_t = r_t * state.sum(-1)
                return (state, out_t)
            seq = (jnp.moveaxis(w, 1, 0), jnp.moveaxis(k, 1, 0), jnp.moveaxis(v, 1, 0), jnp.moveaxis(r, 1, 0))
            state0 = jnp.zeros((b, nh, hd, hd), dtype=x.dtype)
            _, outs = jax.lax.scan(step, state0, seq)
            out = jnp.moveaxis(outs, 0, 1).reshape(b, t, d)
            eps = jnp.asarray(jnp.finfo(out.dtype).eps, out.dtype)
            out = out * jax.lax.rsqrt(jnp.mean(out * out, axis=-1, keepdims=True) + eps)
            return out @ Wo.T
        key = jax.random.key(seed)
        ks = jax.random.split(key, 6)
        scale = 0.02
        x = jax.random.normal(ks[0], (B, T, D), dtype=jnp.float32)
        Wr = jax.random.normal(ks[1], (D, D), dtype=jnp.float32) * scale
        Wk = jax.random.normal(ks[2], (D, D), dtype=jnp.float32) * scale
        Wv = jax.random.normal(ks[3], (D, D), dtype=jnp.float32) * scale
        Ww = jax.random.normal(ks[4], (D, D), dtype=jnp.float32) * scale
        Wo = jax.random.normal(ks[5], (D, D), dtype=jnp.float32) * scale
        return {'x': x, 'Wr': Wr, 'Wk': Wk, 'Wv': Wv, 'Ww': Ww, 'Wo': Wo}
    _L0_attn_all = _L0_attn_setup()
    _L0_attn_in = {k: v for k, v in _L0_attn_all.items() if k in ('Wr', 'Wk', 'Wv', 'Ww', 'Wo')}
    del _L0_attn_all

    def _L0_ffn_setup():
        import jax, jax.numpy as jnp
        import numpy as np
        DIM = 256
        HIDDEN = 704
        N_EXPERTS = 8
        TOP_K = 2
        B, S = (4, 512)

        def _ffn(x, w1, w2, w3):
            h = jax.nn.silu(x @ w1.T) * (x @ w3.T)
            return h @ w2.T
        key = jax.random.key(seed)
        ks = jax.random.split(key, 9)
        scale = 1.0 / np.sqrt(DIM)
        x = jax.random.normal(ks[0], (B, S, DIM), dtype=jnp.float32)
        gate_w = jax.random.normal(ks[1], (N_EXPERTS, DIM), dtype=jnp.float32) * scale
        w1 = jax.random.normal(ks[2], (N_EXPERTS, HIDDEN, DIM), dtype=jnp.float32) * scale
        w2 = jax.random.normal(ks[3], (N_EXPERTS, DIM, HIDDEN), dtype=jnp.float32) * (1.0 / np.sqrt(HIDDEN))
        w3 = jax.random.normal(ks[4], (N_EXPERTS, HIDDEN, DIM), dtype=jnp.float32) * scale
        sw1 = jax.random.normal(ks[5], (HIDDEN, DIM), dtype=jnp.float32) * scale
        sw2 = jax.random.normal(ks[6], (DIM, HIDDEN), dtype=jnp.float32) * (1.0 / np.sqrt(HIDDEN))
        sw3 = jax.random.normal(ks[7], (HIDDEN, DIM), dtype=jnp.float32) * scale
        return {'x': x, 'gate_w': gate_w, 'w1': w1, 'w2': w2, 'w3': w3, 'sw1': sw1, 'sw2': sw2, 'sw3': sw3}
    _L0_ffn_all = _L0_ffn_setup()
    _L0_ffn_in = {k: v for k, v in _L0_ffn_all.items() if k in ('gate_w', 'w1', 'w2', 'w3', 'sw1', 'sw2', 'sw3')}
    del _L0_ffn_all
    return {'x': x, 'ctx_1024': ctx_1024, 'L0_attn_Wr': _L0_attn_in['Wr'], 'L0_attn_Wk': _L0_attn_in['Wk'], 'L0_attn_Wv': _L0_attn_in['Wv'], 'L0_attn_Ww': _L0_attn_in['Ww'], 'L0_attn_Wo': _L0_attn_in['Wo'], 'L0_ffn_gate_w': _L0_ffn_in['gate_w'], 'L0_ffn_w1': _L0_ffn_in['w1'], 'L0_ffn_w2': _L0_ffn_in['w2'], 'L0_ffn_w3': _L0_ffn_in['w3'], 'L0_ffn_sw1': _L0_ffn_in['sw1'], 'L0_ffn_sw2': _L0_ffn_in['sw2'], 'L0_ffn_sw3': _L0_ffn_in['sw3']}

def reference(x, ctx_1024, L0_attn_Wr, L0_attn_Wk, L0_attn_Wv, L0_attn_Ww, L0_attn_Wo, L0_ffn_gate_w, L0_ffn_w1, L0_ffn_w2, L0_ffn_w3, L0_ffn_sw1, L0_ffn_sw2, L0_ffn_sw3):
    import jax
    import jax.numpy as jnp

    def _L0_xattn_ref(teacher_features, student_features):
        import jax, jax.numpy as jnp
        import numpy as np
        from jax import lax
        BIG = jnp.float32(1e+30)

        def _pairwise_euclidean(a, b):
            aa = jnp.sum(a * a, axis=-1)[:, None]
            bb = jnp.sum(b * b, axis=-1)[None, :]
            ab = a @ b.T
            return jnp.sqrt(jnp.maximum(aa + bb - 2.0 * ab, 0.0))

        def _dtw_cost(D):
            row0 = jnp.cumsum(D[0])

            def row_step(prev_row, d_row):
                first = d_row[0] + prev_row[0]

                def col_step(left, inp):
                    d_ij, up, diag = inp
                    r = d_ij + jnp.minimum(jnp.minimum(up, left), diag)
                    return (r, r)
                _, rest = lax.scan(col_step, first, (d_row[1:], prev_row[1:], prev_row[:-1]))
                row = jnp.concatenate([first[None], rest])
                return (row, row)
            _, rows = lax.scan(row_step, row0, D[1:])
            return jnp.concatenate([row0[None], rows], axis=0)

        def _backtrack(R, T1, T2):
            L = T1 + T2 - 1

            def step(carry, _):
                i, j, done = carry
                valid = jnp.logical_not(done)
                cd = jnp.where((i > 0) & (j > 0), R[jnp.maximum(i - 1, 0), jnp.maximum(j - 1, 0)], BIG)
                cu = jnp.where(i > 0, R[jnp.maximum(i - 1, 0), j], BIG)
                cl = jnp.where(j > 0, R[i, jnp.maximum(j - 1, 0)], BIG)
                choice = jnp.argmin(jnp.stack([cd, cu, cl]))
                ni = jnp.where(choice <= 1, i - 1, i)
                nj = jnp.where((choice == 0) | (choice == 2), j - 1, j)
                at_origin = (i == 0) & (j == 0)
                ni = jnp.where(at_origin, 0, ni)
                nj = jnp.where(at_origin, 0, nj)
                return ((ni, nj, done | at_origin), (i, j, valid))
            init = (jnp.int32(T1 - 1), jnp.int32(T2 - 1), jnp.bool_(False))
            _, (i_idx, j_idx, valid) = lax.scan(step, init, None, length=L)
            return (i_idx, j_idx, valid)

        def _align_one(small, large):
            T_small, d = small.shape
            T_large = large.shape[0]
            D = _pairwise_euclidean(small, large)
            R = _dtw_cost(D)
            i_idx, j_idx, valid = _backtrack(R, T_small, T_large)
            contrib = small[i_idx] * valid[:, None].astype(small.dtype)
            expanded = jnp.zeros((T_large, d), dtype=small.dtype).at[j_idx].add(contrib)
            return expanded
        return jax.vmap(_align_one)(teacher_features, student_features)

    def _L0_attn_ref(x, Wr, Wk, Wv, Ww, Wo):
        import jax, jax.numpy as jnp
        import numpy as np
        B, T, D, NH = (4, 512, 256, 16)
        HD = D // NH

        def _rwkv7_forward(x, Wr, Wk, Wv, Ww, Wo):
            b, t, d = x.shape
            nh, hd = (NH, d // NH)
            r = jax.nn.sigmoid(x @ Wr.T).reshape(b, t, nh, hd)
            k = (x @ Wk.T).reshape(b, t, nh, hd)
            v = (x @ Wv.T).reshape(b, t, nh, hd)
            w = (jax.nn.sigmoid(x @ Ww.T) * 0.99).reshape(b, t, nh, hd)

            def step(state, inp):
                w_t, k_t, v_t, r_t = inp
                state = state * w_t[..., :, None] + v_t[..., :, None] * k_t[..., None, :]
                out_t = r_t * state.sum(-1)
                return (state, out_t)
            seq = (jnp.moveaxis(w, 1, 0), jnp.moveaxis(k, 1, 0), jnp.moveaxis(v, 1, 0), jnp.moveaxis(r, 1, 0))
            state0 = jnp.zeros((b, nh, hd, hd), dtype=x.dtype)
            _, outs = jax.lax.scan(step, state0, seq)
            out = jnp.moveaxis(outs, 0, 1).reshape(b, t, d)
            eps = jnp.asarray(jnp.finfo(out.dtype).eps, out.dtype)
            out = out * jax.lax.rsqrt(jnp.mean(out * out, axis=-1, keepdims=True) + eps)
            return out @ Wo.T
        return _rwkv7_forward(x, Wr, Wk, Wv, Ww, Wo)

    def _L0_ffn_ref(x, gate_w, w1, w2, w3, sw1, sw2, sw3):
        import jax, jax.numpy as jnp
        import numpy as np
        DIM = 256
        HIDDEN = 704
        N_EXPERTS = 8
        TOP_K = 2
        B, S = (4, 512)

        def _ffn(x, w1, w2, w3):
            h = jax.nn.silu(x @ w1.T) * (x @ w3.T)
            return h @ w2.T
        Bx, Sx, D = x.shape
        xf = x.reshape(-1, D)
        logits = xf @ gate_w.T
        scores = jax.nn.softmax(logits, axis=-1)
        topk_scores, topk_idx = jax.lax.top_k(scores, TOP_K)
        topk_scores = topk_scores / (jnp.sum(topk_scores, axis=-1, keepdims=True) + 1e-20)
        y = jnp.zeros_like(xf)
        for e in range(N_EXPERTS):
            we = jnp.sum(jnp.where(topk_idx == e, topk_scores, 0.0), axis=-1)
            y = y + we[:, None] * _ffn(xf, w1[e], w2[e], w3[e])
        y = y.reshape(Bx, Sx, D)
        return y + _ffn(x, sw1, sw2, sw3)
    x = x + _L0_xattn_ref(ctx_1024, _layernorm(x, axis=-1))
    x = x + _L0_attn_ref(_layernorm(x, axis=-1), L0_attn_Wr, L0_attn_Wk, L0_attn_Wv, L0_attn_Ww, L0_attn_Wo)
    x = x + _L0_ffn_ref(_layernorm(x, axis=-1), L0_ffn_gate_w, L0_ffn_w1, L0_ffn_w2, L0_ffn_w3, L0_ffn_sw1, L0_ffn_sw2, L0_ffn_sw3)
    return x

_drawn_inputs = setup_inputs


def setup_inputs(seed=0):
    import zlib

    import numpy as np

    out = dict(_drawn_inputs(seed))
    spreads = {}
    factors = {'L0_attn_Wr': 8.0,
     'L0_attn_Wk': 8.0,
     'L0_attn_Wv': 8.0,
     'L0_attn_Ww': 8.0,
     'L0_attn_Wo': 8.0,
     'L0_ffn_gate_w': 8.0,
     'L0_ffn_w1': 8.0,
     'L0_ffn_w2': 8.0,
     'L0_ffn_w3': 8.0,
     'L0_ffn_sw1': 8.0,
     'L0_ffn_sw2': 8.0,
     'L0_ffn_sw3': 8.0}
    for name, (base, spread) in spreads.items():
        noise = np.random.default_rng([zlib.crc32(name.encode()), seed]).standard_normal(out[name].shape)
        drawn = base * np.exp(spread * noise) if base else spread * noise
        out[name] = jnp.asarray(drawn.astype(out[name].dtype))
    for name, factor in factors.items():
        out[name] = (out[name] * factor).astype(out[name].dtype)
    return out
```

```python
from contextlib import ExitStack

import numpy as np
import concourse.bass as bass
from concourse import mybir

F32 = mybir.dt.float32
I32 = mybir.dt.int32
U32 = mybir.dt.uint32
ALU = mybir.AluOpType
ACT = mybir.ActivationFunctionType
AX = mybir.AxisListType

P = 128
B, T, D = 32, 64, 256
N = 1601
KC = D // P
TILES = B * T // P
SEGS = 8
L = -(-N // SEGS)
GB = P // SEGS
GROUPS = B // GB
STEPS = T + SEGS - 1
SLOTS = STEPS + 1
W = L + 1
BIG = 1e30
QC = 2 * L
QUARTERS = SEGS // 2
HC = 2 * QC
CT = -(-N // P)
HEADS, HD = 16, 16
CH = 512
CHUNKS = B * T // CH
CTILES = CH // P
E, HID = 8, 704
HK = -(-HID // P)
EPS_LN = 1e-5
EPS_RMS = float(np.finfo(np.float32).eps)
TIE = -2e-37
HALF_RSQRT_MAGIC = float(0x5F3759DF - 0x00800000)


class Tick:
    def __init__(self, sem, value):
        self.sem, self.value = sem, value


class Lane:
    def __init__(self, engine, sem):
        self.engine, self.sem, self.count, self.seen = engine, sem, 0, {}

    def wait(self, *ticks):
        for t in ticks:
            if t is not None and self.seen.get(t.sem.name, 0) < t.value:
                self.seen[t.sem.name] = t.value
                self.engine.wait_ge(t.sem, t.value)

    def do(self, op, *waits):
        self.wait(*waits)
        self.count += 1
        op(self.engine).then_inc(self.sem, 1)
        return Tick(self.sem, self.count)

    def more(self, op, *waits):
        self.wait(*waits)
        op(self.engine)


class Slot:
    def __init__(self, sem):
        self.sem, self.count = sem, 0

    def dma(self, lane, out, in_, *waits):
        lane.wait(*waits)
        self.count += 16
        lane.engine.dma_start(out, in_).then_inc(self.sem, 16)
        return Tick(self.sem, self.count)


def bc(ap, n, at):
    ap = ap.unsqueeze(at)
    return ap.to_broadcast([n if k == at else s for k, s in enumerate(ap.shape)])


def build(nc, x, ctx_nat, ctx_tr, wr_t, wk, wv_t, ww_t, wo_t, gate_t, w1_t, w3_t, w2_t, out):
    stack = ExitStack()
    with stack:
        sem = lambda name: stack.enter_context(nc.semaphore(name))
        psum = [stack.enter_context(nc.psum_tensor(f"bank{i}", [P, 512], F32)) for i in range(8)]
        pe, dve, act, pool, sp = (Lane(engine, sem(f"{n}_done")) for engine, n in (
            (nc.tensor, "pe"), (nc.vector, "dve"), (nc.scalar, "act"), (nc.gpsimd, "pool"), (nc.sync, "sp")))

        top = [nc.sbuf_base + (-nc.sbuf_base) % 32]

        def place(name, free, offset=None, dt=F32):
            size = int(np.prod(free)) * 4
            at = top[0] if offset is None else offset
            if offset is None:
                top[0] += size + (-size) % 32
            assert at + size <= nc.sbuf_usable_end, (name, at + size, nc.sbuf_usable_end)
            return nc.alloc_sbuf_tensor_at(name, [P] + list(free), dt, offset=at)

        def region(size):
            at = top[0]
            top[0] += size + (-size) % 32
            return at

        ident = place("ident", [P])
        ones = place("ones", [T])
        row1 = place("row1", [L])
        rowP = place("rowP", [CT])
        lane_i = place("lane_i", [1], dt=I32)
        seg_i = place("seg_i", [1], dt=I32)
        seg = place("seg", [1])
        first_big = place("first_big", [1])
        start = place("start", [1])
        not_last = place("not_last", [1])
        inject = place("inject", [STEPS])
        step_io = place("step_io", [STEPS])
        expert_io = place("expert_io", [E])
        blocks = place("blocks", [P])
        bb = place("bb", [TILES])
        threshold = [place(f"threshold{g}", [SLOTS]) for g in range(GROUPS)]
        stats = place("stats", [4, 6])
        mv = place("mv", [TILES, 2])
        ln_a, ln_b, ln_c, ln_d = (place(f"ln_{c}", [TILES]) for c in "abcd")
        latT = place("latT", [KC, B * T])
        h2T = latT

        DPB = SLOTS * W * 4
        dp_at = [region(DPB) for _ in range(GROUPS)]
        table = [place(f"table{g}", [SLOTS, W], dp_at[g]) for g in range(GROUPS)]
        work_at = top[0]

        ctxT = [place(f"ctxT{i}", [2, KC, HC]) for i in range(2)]
        sq = [place(f"sq{i}", [2, KC, QC]) for i in range(2)]
        sqs = [place(f"sqs{i}", [2, QC]) for i in range(2)]
        z = [place(f"z{i}", [QC]) for i in range(2)]
        root = [place(f"root{i}", [QC]) for i in range(2)]
        root2 = [place(f"root2{i}", [QC]) for i in range(2)]
        slope = place("slope", [QC])
        dist = [place(f"dist{i}", [QC]) for i in range(2)]
        col_min = place("col_min", [L])
        above = place("above", [L])
        across = place("across", [L])
        is_diag = place("is_diag", [L])
        row_code = place("row_code", [L])
        shifted = place("shifted", [1])
        best = place("best", [L])
        reach = place("reach", [1])

        lat = place("lat", [TILES, D], dp_at[1])
        latn = place("latn", [TILES, D], dp_at[1] + TILES * D * 4)

        c_ident0 = pool.do(lambda e: e.memset(ident[:, :], 0.0))
        c_ident = pool.do(lambda e: e.affine_select(out=ident[:, :], in_=ident[:, :], compare_op=ALU.not_equal, fill=1.0,
                                                    base=0, pattern=[[-1, P]], channel_multiplier=1), c_ident0)
        c_lane = pool.do(lambda e: e.iota(lane_i[:, :], [[0, 1]], base=0, channel_multiplier=1))
        c_rowP = pool.do(lambda e: e.iota(rowP[:, :], [[P, CT]], base=1, channel_multiplier=1,
                                          allow_small_or_imprecise_dtypes=True))
        c_row = pool.do(lambda e: e.iota(row1[:, :], [[1, L]], base=1, channel_multiplier=0,
                                         allow_small_or_imprecise_dtypes=True))
        c_step = pool.do(lambda e: e.iota(step_io[:, :], [[1, STEPS]], base=0, channel_multiplier=0,
                                          allow_small_or_imprecise_dtypes=True))
        c_expert = pool.do(lambda e: e.iota(expert_io[:, :], [[1, E]], base=0, channel_multiplier=0,
                                            allow_small_or_imprecise_dtypes=True))
        c_b0 = pool.do(lambda e: e.memset(blocks[:, :], 1.0))
        heads_view = blocks[:, :].rearrange("p (h c) -> p h c", c=HD)
        c_b1 = pool.do(lambda e: e.affine_select(out=heads_view, in_=heads_view, compare_op=ALU.is_ge, fill=0.0, base=0,
                                                 pattern=[[-HD, P // HD], [0, HD]], channel_multiplier=1), c_b0)
        c_blocks = pool.do(lambda e: e.affine_select(out=heads_view, in_=heads_view, compare_op=ALU.is_ge, fill=0.0,
                                                     base=HD - 1, pattern=[[HD, P // HD], [0, HD]],
                                                     channel_multiplier=-1), c_b1)
        c_ones = dve.do(lambda e: e.memset(ones[:, :], 1.0))
        t0 = dve.do(lambda e: e.tensor_single_scalar(seg_i[:, :], lane_i[:, :], SEGS - 1, ALU.bitwise_and), c_lane)
        c_seg = dve.do(lambda e: e.tensor_copy(seg[:, :], seg_i[:, :]), t0)
        c_first = dve.do(lambda e: e.tensor_scalar(first_big[:, :], seg[:, :], 0.0, BIG, ALU.is_equal, ALU.mult), c_seg)
        c_start = dve.do(lambda e: e.tensor_scalar(start[:, :], seg[:, :], 0.0, BIG, ALU.is_gt, ALU.mult), c_seg)
        c_nlast = dve.do(lambda e: e.tensor_single_scalar(not_last[:, :], seg[:, :], float(SEGS - 1), ALU.is_lt), c_seg)
        t1 = dve.do(lambda e: e.tensor_scalar(shifted[:, :], seg[:, :], float(L), None, ALU.mult), c_seg)
        c_row1 = dve.do(lambda e: e.tensor_scalar(row1[:, :], row1[:, :], shifted[:, 0:1], None, ALU.add), t1, c_row)
        t2 = dve.do(lambda e: e.tensor_scalar(step_io[:, :], step_io[:, :], seg[:, 0:1], None, ALU.subtract), c_seg, c_step)
        c_inject = dve.do(lambda e: e.tensor_scalar(inject[:, :], step_io[:, :], float(T), float(N), ALU.is_ge, ALU.mult), t2)

        def layer_norm(src, dst, n, ready):
            stats_free = last = None
            for t in range(n):
                s = dve.do(lambda e, t=t: e.bn_stats(stats[:, t % 4, :], src[:, t, :]), *ready)
                last = dve.do(lambda e, t=t: e.bn_aggr(mv[:, t, :], stats[:, t % 4, :]), s)
            v, r, a, c, d = mv[:, 0:n, 1], ln_a[:, 0:n], ln_b[:, 0:n], ln_c[:, 0:n], ln_d[:, 0:n]
            k = dve.do(lambda e: e.tensor_scalar(a, v, EPS_LN, None, ALU.add), last)
            k1 = act.do(lambda e: e.activation(r, a, ACT.Sqrt), k)
            k2 = dve.do(lambda e: e.reciprocal(c, r), k1)
            k3 = dve.do(lambda e: e.tensor_tensor(d, r, r, ALU.mult), k1)
            k4 = dve.do(lambda e: e.tensor_tensor(d, a, d, ALU.subtract), k3)
            k5 = dve.do(lambda e: e.scalar_tensor_tensor(d, d, 0.5, c, ALU.mult, ALU.mult), k4, k2)
            k6 = dve.do(lambda e: e.tensor_tensor(r, r, d, ALU.add), k5)
            k7 = dve.do(lambda e: e.reciprocal(c, r), k6)
            dve.wait(k7)
            for t in range(n):
                last = dve.do(lambda e, t=t: e.tensor_scalar(dst[:, t, :], src[:, t, :], mv[:, t, 0:1], ln_c[:, t:t + 1],
                                                             ALU.subtract, ALU.mult))
            return last

        x_tiles = x.rearrange("b t d -> (b t) d").rearrange("(n p) d -> p n d", p=P)
        lat_in = Slot(sem("lat_in"))
        got_lat = lat_in.dma(sp, lat[:, :, :], x_tiles)
        lat_done = layer_norm(lat, latn, TILES, [got_lat])
        norm_sq = None
        for t in range(TILES):
            norm_sq = act.do(lambda e, t=t: e.activation(lat[:, t, :], latn[:, t, :], ACT.Square,
                                                         accum_out=bb[:, t:t + 1]), lat_done)

        bank_free = [None] * 8

        def transpose_tiles(src, dst, t0, scale, ready, bank):
            for k in range(KC):
                for j in range(2):
                    w = ready if (k, j) == (0, 0) else ()
                    op = lambda e, k=k, j=j: e.transpose(psum[bank][:, (2 * k + j) * P:(2 * k + j + 1) * P],
                                                         src[:, t0 + j, k * P:(k + 1) * P], ident[:, :])
                    if (k, j) == (KC - 1, 1):
                        tr = pe.do(op, *w)
                    else:
                        pe.more(op, *w, *((bank_free[bank],) if (k, j) == (0, 0) else ()))
            bank_free[bank] = act.do(lambda e: e.activation(dst[:, :, t0 * P:(t0 + 2) * P],
                                                            psum[bank][:, :].rearrange("p (k n) -> p k n", k=KC),
                                                            ACT.Copy, scale=scale), tr)
            return bank_free[bank]

        for t in range(0, TILES, 2):
            latT_done = transpose_tiles(latn, latT, t, -2.0, [lat_done, c_ident], t // 2 % 2)
        prologue_done = [norm_sq, latT_done, lat_done]

        ctxT_in = [Slot(sem(f"ctxT_in{i}")) for i in range(2)]
        ctxT_free = [[], []]
        ctxT_got = {}
        dist_out = [Slot(sem(f"dist_out{i}")) for i in range(2)]
        dist_sent = [None, None]
        ring = dict(sq=[None, None], sqs=[None, None], z=[None, None], root=[None, None], root2=[None, None], slope=None)
        table_ready = {}

        def load_ctxT(n):
            if n >= 2 * TILES:
                return
            pair, half = divmod(n, 2)
            c0, c1 = half * HC, min(N, (half + 1) * HC)
            for b in range(2):
                ctxT_got[n] = ctxT_in[n % 2].dma(
                    sp, ctxT[n % 2][:, b, :, 0:c1 - c0],
                    ctx_tr[2 * pair + b].rearrange("(k p) i -> p k i", p=P)[:, :, c0:c1], *ctxT_free[n % 2])
            ctxT_free[n % 2] = []

        def clear_table(g, ready):
            tb = table[g]
            a = pool.do(lambda e: e.memset(tb[:, 0:SEGS, :], BIG), *ready)
            b = pool.do(lambda e: e.memset(tb[:, T + 1:SLOTS, :], BIG))
            c = pool.do(lambda e: e.memset(tb[:, SEGS:T + 1, 1 + N - (SEGS - 1) * L:W], BIG))
            d = pool.do(lambda e: e.memset(tb[:, SEGS:T + 1, 0:1], BIG))
            return [a, b, c, d]

        def squares(u):
            n, q = divmod(u, 2)
            nq = min(N, (u % QUARTERS + 1) * QC) - u % QUARTERS * QC
            i = u % 2
            view = ctxT[n % 2][:, :, :, q * QC:q * QC + nq]
            s = act.do(lambda e: e.activation(sq[i][:, :, :, 0:nq], view, ACT.Square), ctxT_got[n], ring["sq"][i])
            ring["sq"][i] = pool.do(lambda e: e.tensor_tensor(sqs[i][:, :, 0:nq], sq[i][:, :, 0, 0:nq], sq[i][:, :, 1, 0:nq],
                                                              ALU.add), s, ring["sqs"][i])
            return s, ring["sq"][i]

        def distance_unit(u, sq_ticks, cleared):
            n, half = divmod(u, 2)
            pair, q = divmod(u, QUARTERS)
            nq = min(N, (q + 1) * QC) - q * QC
            i, bank = u % 2, u % 3
            ps = psum[bank]
            pe.wait(ctxT_got[n], bank_free[bank], *prologue_done, c_ones)
            for b in range(2):
                for k in range(KC):
                    tick = pe.do(lambda e, b=b, k=k: e.matmul(
                        ps[b * T:(b + 1) * T, 0:nq], latT[:, k, pair * P + b * T:pair * P + (b + 1) * T],
                        ctxT[n % 2][:, b, k, half * QC:half * QC + nq], start=(k == 0), stop=False))
            read_ctxT = tick
            for b in range(2):
                tick = pe.do(lambda e, b=b: e.matmul(ps[b * T:(b + 1) * T, 0:nq], ones[:, 0:T], sqs[i][:, b, 0:nq],
                                                     start=False, stop=True), sq_ticks[1])
            ring["sqs"][i] = tick
            ctxT_free[n % 2] = [read_ctxT, sq_ticks[0]]
            if half:
                load_ctxT(n + 2)
            zi, ri, r2, di = z[i][:, 0:nq], root[i][:, 0:nq], root2[i][:, 0:nq], dist[i][:, 0:nq]
            z_done = dve.do(lambda e: e.tensor_scalar(zi, ps[:, 0:nq], bb[:, pair:pair + 1], 1e-30, ALU.add, ALU.max),
                            tick, ring["z"][i])
            bank_free[bank] = z_done
            root_done = act.do(lambda e: e.activation(ri, zi, ACT.Sqrt), z_done, ring["root"][i])
            sq_done = act.do(lambda e: e.activation(r2, ri, ACT.Square), root_done, ring["root2"][i])
            slope_done = dve.do(lambda e: e.tensor_scalar(slope[:, 0:nq].bitcast(I32), zi.bitcast(I32), -0.5,
                                                          HALF_RSQRT_MAGIC, ALU.mult, ALU.add), z_done, ring["slope"])
            err = dve.do(lambda e: e.tensor_tensor(zi, zi, r2, ALU.subtract), sq_done, slope_done)
            ring["root2"][i] = err
            corr = dve.do(lambda e: e.tensor_tensor(zi, zi, slope[:, 0:nq], ALU.mult), err)
            ring["slope"] = corr
            done = dve.do(lambda e: e.tensor_tensor(di, ri, zi, ALU.add), corr, dist_sent[i])
            ring["z"][i] = ring["root"][i] = done
            g = pair * 2 // GB
            for b in range(2):
                for s in range(2):
                    m = min(L, nq - s * L)
                    sg = 2 * q + s
                    part = (2 * pair + b) % GB * SEGS + sg
                    dist_sent[i] = dist_out[i].dma(
                        sp, table[g][part:part + 1, 1 + sg:1 + sg + T, 1:1 + m],
                        dist[i][b * T:(b + 1) * T, s * L:s * L + m], done, *cleared)

        def distances(g, cleared):
            units = range(g * QUARTERS * TILES // GROUPS, (g + 1) * QUARTERS * TILES // GROUPS)
            sq_ticks = squares(units[0])
            for u in units:
                ahead = squares(u + 1) if u + 1 in units and (u + 1) // 2 in ctxT_got else None
                distance_unit(u, sq_ticks, cleared)
                if u + 1 in units:
                    sq_ticks = ahead or squares(u + 1)
                yield
            table_ready[g] = list(dist_sent)

        down = [31] + list(range(31))
        upwards = list(range(1, 32)) + [0]
        dtw = dict(shift=None, last=None, codes=None)
        path_ready = {}

        def align(g):
            tb = table[g]
            ready = table_ready[g] + [c_first, c_start, c_row1, c_inject, c_nlast]
            dve.wait(*ready)
            pool.wait(*ready)
            row_free = {}
            halo = None
            code_read = None
            for step in range(STEPS):
                prev, cur = tb[:, step, :], tb[:, step + 1, :]
                left, diag, up = prev[:, 1:W], prev[:, 0:L], cur[:, 0:L]
                m = dve.do(lambda e: e.tensor_tensor(col_min[:, :], left, diag, ALU.min), halo, dtw["last"])
                first = start[:, 0:1] if step == 0 else cur[:, 0:1]
                cost = dve.do(lambda e, first=first: e.tensor_tensor_scan(cur[:, 1:W], col_min[:, :], cur[:, 1:W], first,
                                                                         ALU.min, ALU.add), m, halo)
                if step + 1 < STEPS:
                    nxt = tb[:, step + 2, :]
                    sh = dve.do(lambda e: e.stream_shuffle(shifted[:, 0:1], cur[:, L:W], down), cost, dtw["shift"])
                    halo_next = dve.do(lambda e: e.tensor_scalar(nxt[:, 0:1], shifted[:, 0:1], first_big[:, 0:1], None,
                                                                 ALU.max), sh)
                    dtw["shift"] = halo_next
                free = dtw["codes"]
                gain = pool.do(lambda e: e.tensor_tensor(above[:, :], up, col_min[:, :], ALU.subtract), cost, halo, free)
                side = pool.do(lambda e: e.tensor_tensor(across[:, :], left, diag, ALU.subtract))
                half = dve.do(lambda e: e.tensor_scalar(is_diag[:, :], across[:, :], 0.0, -0.5, ALU.is_ge, ALU.mult), side)
                rc = pool.do(lambda e: e.tensor_tensor(row_code[:, :], row1[:, :], is_diag[:, :], ALU.add), half)
                tied = dve.do(lambda e: e.scalar_tensor_tensor(above[:, :], is_diag[:, :], TIE, above[:, :],
                                                               ALU.mult, ALU.add), half, gain)
                dtw["last"] = dve.do(lambda e: e.scalar_tensor_tensor(left, above[:, :], 0.0, row_code[:, :],
                                                                      ALU.is_gt, ALU.mult), tied, rc)
                dtw["codes"] = dtw["last"]
                if step + 1 < STEPS:
                    halo = halo_next
                yield
            th = threshold[g]
            t_old = dve.do(lambda e: e.memset(th[:, STEPS:SLOTS], float(N)), dtw["last"])
            for step in range(STEPS - 1, -1, -1):
                code, old, new = tb[:, step, 1:W], th[:, step + 1:step + 2], th[:, step:step + 1]
                a = dve.do(lambda e: e.scalar_tensor_tensor(best[:, :], row1[:, :], old, code, ALU.is_le, ALU.mult), t_old)
                s = dve.do(lambda e: e.stream_shuffle(shifted[:, 0:1], old, upwards), dtw["shift"], t_old)
                r = dve.do(lambda e: e.tensor_reduce(reach[:, 0:1], best[:, :], AX.X, ALU.max), a)
                t_old = dve.do(lambda e: e.scalar_tensor_tensor(new, shifted[:, 0:1], not_last[:, 0:1], reach[:, 0:1],
                                                                ALU.mult, ALU.max), s, r)
                dtw["shift"] = t_old
                if step >= T:
                    t_old = dve.do(lambda e: e.tensor_tensor(new, new, inject[:, step:step + 1], ALU.max), t_old)
                yield
            path_ready[g] = t_old

        cleared0 = clear_table(0, [])
        load_ctxT(0)
        load_ctxT(1)
        for _ in distances(0, cleared0):
            pass
        cleared1 = clear_table(1, prologue_done)
        steps = align(0)
        for n, _ in enumerate(distances(1, cleared1)):
            for _ in range(4):
                next(steps, None)
        for _ in steps:
            pass
        for _ in align(1):
            pass

        distance_done = list(bank_free) + [Tick(pe.sem, pe.count)]
        dve_then, act_then, pe_then, pool_then = (Tick(l.sem, l.count) for l in (dve, act, pe, pool))
        after_dtw = [dve_then, act_then, pe_then, pool_then] + [Tick(d.sem, d.count) for d in dist_out]

        top[0] = dp_at[0]
        xr = place("xr", [TILES, D])
        rows_c = [place(f"rows_c{i}", [CT, D]) for i in range(3)]
        on_path = [place(f"on_path{i}", [CT, T]) for i in range(2)]
        below = [place(f"below{i}", [CT, T]) for i in range(2)]
        cuts = [place(f"cuts{i}", [T + 1]) for i in range(2)]
        work2_at = top[0]

        x_in = Slot(sem("x_in"))
        got_x = x_in.dma(sp, xr[:, :, :], x_tiles, *after_dtw)
        rows_in = [Slot(sem(f"rows_in{i}")) for i in range(3)]
        rows_free, rows_got = [list(after_dtw)] * 3, {}

        def load_rows(b):
            if b >= B:
                return
            i = b % 3
            full = (N // P) * P
            rows_in[i].dma(sp, rows_c[i][:, 0:N // P, :], ctx_nat[b, 0:full, :].rearrange("(t p) d -> p t d", p=P),
                           *rows_free[i])
            rows_got[b] = rows_in[i].dma(sp, rows_c[i][0:N - full, N // P, :], ctx_nat[b, full:N, :])

        for b in range(3):
            load_rows(b)
        path_free, below_free, cuts_free = [None] * 2, [None] * 2, [None] * 2
        added = []
        for b in range(B):
            g, i, j = b // GB, b % 2, b % 3
            bank = 2 + i
            row = b % GB * SEGS
            tc_ = pe.do(lambda e: e.matmul(psum[bank][:, 0:T + 1], ident[:, row:row + 1].to_broadcast([P, P]),
                                           threshold[g][:, 0:T + 1], start=True, stop=True),
                        bank_free[bank], path_ready[g], *after_dtw)
            cd = act.do(lambda e: e.activation(cuts[i][:, :], psum[bank][:, 0:T + 1], ACT.Copy), tc_, cuts_free[i])
            bank_free[bank] = cd
            rp = bc(rowP[:, :], T, 2)
            lo, hi = bc(cuts[i][:, 0:T], CT, 1), bc(cuts[i][:, 1:T + 1], CT, 1)
            a = dve.do(lambda e: e.tensor_tensor(on_path[i][:, :, :], rp, lo, ALU.is_ge), cd, path_free[i], c_rowP)
            h = dve.do(lambda e: e.tensor_tensor(below[i][:, :, :], rp, hi, ALU.is_le), below_free[i])
            cuts_free[i] = h
            below_free[i] = pool.do(lambda e: e.tensor_tensor(on_path[i][:, :, :], on_path[i][:, :, :], below[i][:, :, :],
                                                              ALU.mult), a, h)
            pb = b // 2 % 2
            half = b % 2
            for t in range(CT):
                k = min(P, N - t * P)
                pe.more(lambda e, t=t, k=k: e.matmul(psum[pb][half * T:(half + 1) * T, 0:D], on_path[i][0:k, t, :],
                                                     rows_c[j][0:k, t, :], start=(t == 0), stop=(t == CT - 1)),
                        below_free[i], rows_got[b], bank_free[pb]) if t < CT - 1 else None
            t, k = CT - 1, N - (CT - 1) * P
            ex = pe.do(lambda e: e.matmul(psum[pb][half * T:(half + 1) * T, 0:D], on_path[i][0:k, t, :],
                                          rows_c[j][0:k, t, :], start=False, stop=True))
            path_free[i] = ex
            rows_free[j] = [ex]
            load_rows(b + 3)
            if half:
                bank_free[pb] = dve.do(lambda e: e.tensor_tensor(xr[:, b // 2, :], xr[:, b // 2, :], psum[pb][:, 0:D],
                                                                 ALU.add), ex, got_x)
                added.append(bank_free[pb])

        top[0] = work2_at
        w_r, w_k, w_v, w_w, w_o, w_ks = (place(n, [KC, D]) for n in ("w_r", "w_k", "w_v", "w_w", "w_o", "w_ks"))
        w_g = place("w_g", [KC, E])
        hn = place("hn", [CTILES, D])
        hT = place("hT", [KC, CH])
        gate_r, decay, val, kv, state, mix = (place(n, [KC, CH]) for n in ("gate_r", "decay", "val", "kv", "state", "mix"))
        mix2 = val
        rms, rms2 = place("rms", [CTILES]), place("rms2", [CTILES])
        lg, sc, top8 = place("lg", [TILES, E]), place("sc", [TILES, E]), place("top8", [TILES, 8])
        top8b, idx = place("top8b", [TILES, 8]), place("idx", [TILES, 8], dt=U32)
        idxf, den, share = place("idxf", [TILES, 2]), place("den", [TILES]), place("share", [TILES, E])
        pick = place("pick", [TILES, E])
        ssum = place("ssum", [TILES])
        work3_at = top[0]
        rec_in = Slot(sem("rec_in"))
        for tile_, src in ((w_r, wr_t), (w_k, wk), (w_v, wv_t), (w_w, ww_t), (w_o, wo_t), (w_g, gate_t)):
            got_rec = rec_in.dma(sp, tile_[:, :, :], src.rearrange("(k p) n -> p k n", p=P), *after_dtw)
        for k in range(KC):
            for oc in range(KC):
                tk = pe.do(lambda e, k=k, oc=oc: e.matmul(psum[2 + k][:, oc * P:(oc + 1) * P], w_k[:, oc, k * P:(k + 1) * P],
                                                          blocks[:, :], start=True, stop=True),
                           got_rec, c_blocks, bank_free[2 + k])
            ks_done = bank_free[2 + k] = act.do(lambda e, k=k: e.activation(w_ks[:, k, :], psum[2 + k][:, 0:D], ACT.Copy), tk)

        rec = dict(hn=None, hT=None, r=None, w=None, v=None, kv=None, st=None, mix=None, m2=None, rms=None)
        nat_done = []
        for c in range(CHUNKS):
            t0 = c * CTILES
            y_done = layer_norm(xr[:, t0:t0 + CTILES, :], hn, CTILES, [added[t0 + CTILES - 1], rec["hn"]])
            for t in range(0, CTILES, 2):
                rec["hn"] = hT_done = transpose_tiles(hn, hT, t, 1.0, [y_done, rec["hT"]], t // 2)

            def project(w, oc, bank):
                pe.wait(bank_free[bank], hT_done, got_rec, ks_done)
                for k in range(KC):
                    tick = pe.do(lambda e, k=k: e.matmul(psum[bank][:, :], w[:, k, oc * P:(oc + 1) * P], hT[:, k, :],
                                                         start=(k == 0), stop=(k == KC - 1)))
                return tick

            for oc in range(KC):
                p = project(w_r, oc, 2)
                r_done = bank_free[2] = act.do(lambda e: e.activation(gate_r[:, oc, :], psum[2][:, :], ACT.Sigmoid), p, rec["r"])
                p = project(w_w, oc, 3)
                w1d = bank_free[3] = act.do(lambda e: e.activation(decay[:, oc, :], psum[3][:, :], ACT.Sigmoid), p, rec["w"])
                p = project(w_v, oc, 4)
                v_done = bank_free[4] = act.do(lambda e: e.activation(val[:, oc, :], psum[4][:, :], ACT.Copy), p, rec["v"])
                p = project(w_ks, oc, 5)
                kv_done = bank_free[5] = dve.do(lambda e: e.tensor_tensor(kv[:, oc, :], psum[5][:, :], val[:, oc, :], ALU.mult),
                                                p, v_done, rec["kv"])
                w2d = dve.do(lambda e: e.tensor_scalar(decay[:, oc, :], decay[:, oc, :], 0.99, None, ALU.mult), w1d)
                w3d = dve.do(lambda e: e.memset(decay[:, oc, 0:CH:T], 0.0), w2d)
                s_done = dve.do(lambda e: e.tensor_tensor_scan(state[:, oc, :], decay[:, oc, :], kv[:, oc, :], 0.0,
                                                               ALU.mult, ALU.add), w3d, kv_done)
                m_done = dve.do(lambda e: e.tensor_tensor(mix[:, oc, :], gate_r[:, oc, :], state[:, oc, :], ALU.mult),
                                s_done, r_done, rec["mix"])
                m2_done = act.do(lambda e: e.activation(mix2[:, oc, :], mix[:, oc, :], ACT.Square), m_done, kv_done)
            rec["hT"] = p
            rec["r"] = rec["w"] = rec["kv"] = m_done
            for t in range(CTILES):
                for k in range(KC):
                    tk = pe.do(lambda e, t=t, k=k: e.matmul(psum[6][:, t:t + 1], mix2[:, k, t * P:(t + 1) * P], ones[:, 0:1],
                                                            start=(k == 0), stop=(k == KC - 1)), m2_done, bank_free[6])
            rec["v"] = tk
            r1 = bank_free[6] = dve.do(lambda e: e.tensor_scalar(rms[:, :], psum[6][:, 0:CTILES], 1.0 / D, EPS_RMS,
                                                                 ALU.mult, ALU.add), tk, rec["rms"])
            r2 = act.do(lambda e: e.activation(rms2[:, :], rms[:, :], ACT.Sqrt), r1)
            r3 = dve.do(lambda e: e.reciprocal(rms[:, :], rms2[:, :]), r2)
            for t in range(CTILES):
                bank = t % 2
                pe.wait(bank_free[bank], m_done)
                for k in range(KC):
                    tk = pe.do(lambda e, t=t, k=k: e.matmul(psum[bank][:, 0:D], mix[:, k, t * P:(t + 1) * P], w_o[:, k, :],
                                                            start=(k == 0), stop=(k == KC - 1)))
                x_done = bank_free[bank] = dve.do(lambda e, t=t: e.scalar_tensor_tensor(
                    xr[:, t0 + t, :], psum[bank][:, 0:D], rms[:, t:t + 1], xr[:, t0 + t, :], ALU.mult, ALU.add), tk, r3)
            rec["mix"] = tk
            rec["rms"] = x_done
            y_done = layer_norm(xr[:, t0:t0 + CTILES, :], hn, CTILES, [x_done, rec["hn"]])
            for t in range(0, CTILES, 2):
                for_t = t0 + t

                bank = t // 2
                for k in range(KC):
                    for j in range(2):
                        w = (y_done, bank_free[bank])
                        tr = pe.do(lambda e, k=k, j=j: e.transpose(psum[bank][:, (2 * k + j) * P:(2 * k + j + 1) * P],
                                                                   hn[:, t + j, k * P:(k + 1) * P], ident[:, :]), *w)
                rec["hn"] = h2_done = bank_free[bank] = act.do(lambda e, for_t=for_t: e.activation(
                    h2T[:, :, for_t * P:(for_t + 2) * P], psum[bank][:, :].rearrange("p (k n) -> p k n", k=KC), ACT.Copy), tr)
            for t in range(CTILES):
                for k in range(KC):
                    tk = pe.do(lambda e, t=t, k=k: e.matmul(psum[7][:, t * E:(t + 1) * E],
                                                            h2T[:, k, (t0 + t) * P:(t0 + t + 1) * P], w_g[:, k, :],
                                                            start=(k == 0), stop=(k == KC - 1)), h2_done, bank_free[7])
            ts_ = slice(t0, t0 + CTILES)
            g0 = bank_free[7] = dve.do(lambda e: e.tensor_copy(lg[:, ts_, :], psum[7][:, 0:CTILES * E].rearrange(
                "p (t e) -> p t e", e=E)), tk)
            g1 = dve.do(lambda e: e.tensor_reduce(ssum[:, ts_], lg[:, ts_, :], AX.X, ALU.max), g0)
            g2 = dve.do(lambda e: e.tensor_tensor(lg[:, ts_, :], lg[:, ts_, :], bc(ssum[:, ts_], E, 2), ALU.subtract), g1)
            g3 = act.do(lambda e: e.activation(sc[:, ts_, :], lg[:, ts_, :], ACT.Exp), g2)
            g4 = dve.do(lambda e: e.tensor_reduce(ssum[:, ts_], sc[:, ts_, :], AX.X, ALU.add), g3)
            g5 = dve.do(lambda e: e.reciprocal(ssum[:, ts_], ssum[:, ts_]), g4)
            g6 = dve.do(lambda e: e.tensor_tensor(sc[:, ts_, :], sc[:, ts_, :], bc(ssum[:, ts_], E, 2), ALU.mult), g5)
            for t in range(t0, t0 + CTILES):
                m = dve.do(lambda e, t=t: e.max(top8[:, t, :], sc[:, t, :]), g6)
                g7 = dve.do(lambda e, t=t: e.max_index(idx[:, t, :], top8[:, t, :], sc[:, t, :]), m)
            g8 = dve.do(lambda e: e.tensor_copy(idxf[:, ts_, :], idx[:, ts_, 0:2]), g7)
            g9 = dve.do(lambda e: e.scalar_tensor_tensor(den[:, ts_], top8[:, ts_, 0], 1e-20, top8[:, ts_, 1], ALU.add, ALU.add), g7)
            g10 = dve.do(lambda e: e.reciprocal(den[:, ts_], den[:, ts_]), g9)
            g11 = dve.do(lambda e: e.tensor_tensor(top8b[:, ts_, 0:2], top8[:, ts_, 0:2], bc(den[:, ts_], 2, 2), ALU.mult), g10)
            ex_b = bc(expert_io[:, :], CTILES, 1)
            g12 = dve.do(lambda e: e.tensor_tensor(share[:, ts_, :], ex_b, idxf[:, ts_, 0:1].to_broadcast([P, CTILES, E]),
                                                   ALU.is_equal), g8, c_expert)
            g13 = dve.do(lambda e: e.tensor_tensor(share[:, ts_, :], share[:, ts_, :],
                                                   top8b[:, ts_, 0:1].to_broadcast([P, CTILES, E]), ALU.mult), g12, g11)
            g14 = dve.do(lambda e: e.tensor_tensor(pick[:, ts_, :], ex_b, idxf[:, ts_, 1:2].to_broadcast([P, CTILES, E]),
                                                   ALU.is_equal), g13)
            g15 = dve.do(lambda e: e.tensor_tensor(pick[:, ts_, :], pick[:, ts_, :],
                                                   top8b[:, ts_, 1:2].to_broadcast([P, CTILES, E]), ALU.mult), g14)
            share_done = dve.do(lambda e: e.tensor_tensor(share[:, ts_, :], share[:, ts_, :], pick[:, ts_, :], ALU.add), g15)

        top[0] = work3_at
        w_up = [place(f"w_up{i}", [2, KC, HID]) for i in range(2)]
        w_dn = [place(f"w_dn{i}", [HK, D]) for i in range(2)]
        hid = [place(f"hid{i}", [HK, CH]) for i in range(2)]
        act_s = [place(f"act_s{i}", [CH]) for i in range(2)]
        up_in = [Slot(sem(f"up_in{i}")) for i in range(2)]
        w_free, w_got = [[], []], {}
        full = HID // P

        def load_expert(n):
            if n > E:
                return
            i = n % 2
            for m, src in enumerate((w1_t, w3_t)):
                up_in[i].dma(sp, w_up[i][:, m, :, :], src[n].rearrange("(k p) n -> p k n", p=P), *w_free[i], *after_dtw)
            up_in[i].dma(sp, w_dn[i][:, 0:full, :], w2_t[n, 0:full * P, :].rearrange("(k p) n -> p k n", p=P))
            w_got[n] = up_in[i].dma(sp, w_dn[i][0:HID - full * P, full, :], w2_t[n, full * P:HID, :])

        load_expert(0)
        load_expert(1)
        hid_free, act_free = [None, None], [None, None]
        m_, u_ = 0, 0
        for n in range(E + 1):
            i = n % 2
            for c in range(CHUNKS):
                hb = u_ % 2
                u_ += 1
                for hk in range(HK):
                    hs = min(P, HID - hk * P)
                    banks = (m_ % 2, 2 + m_ % 2)
                    a_b = m_ % 2
                    m_ += 1
                    for w in range(2):
                        pe.wait(bank_free[banks[w]], w_got[n], h2_done)
                        for k in range(KC):
                            tk = pe.do(lambda e, w=w, k=k, hk=hk, hs=hs, banks=banks, i=i, c=c: e.matmul(
                                psum[banks[w]][0:hs, :], w_up[i][:, w, k, hk * P:hk * P + hs],
                                h2T[:, k, c * CH:(c + 1) * CH], start=(k == 0), stop=(k == KC - 1)))
                        if w == 0:
                            s_done = bank_free[banks[0]] = act.do(lambda e, hs=hs, a_b=a_b, banks=banks: e.activation(
                                act_s[a_b][0:hs, :], psum[banks[0]][0:hs, :], ACT.Silu), tk, act_free[a_b])
                    u_done = act_free[a_b] = bank_free[banks[1]] = dve.do(
                        lambda e, hs=hs, a_b=a_b, banks=banks, hb=hb, hk=hk: e.tensor_tensor(
                            hid[hb][0:hs, hk, :], psum[banks[1]][0:hs, :], act_s[a_b][0:hs, :], ALU.mult),
                        tk, s_done, hid_free[hb])
                for t in range(CTILES):
                    bank = 4 + t % 4
                    pe.wait(bank_free[bank], u_done)
                    for hk in range(HK):
                        hs = min(P, HID - hk * P)
                        tk = pe.do(lambda e, t=t, hk=hk, hs=hs, hb=hb, bank=bank, i=i: e.matmul(
                            psum[bank][:, 0:D], hid[hb][0:hs, hk, t * P:(t + 1) * P], w_dn[i][0:hs, hk, :],
                            start=(hk == 0), stop=(hk == HK - 1)))
                    tt = c * CTILES + t
                    scale = share[:, tt, n:n + 1] if n < E else 1.0
                    y_done = bank_free[bank] = dve.do(lambda e, tt=tt, scale=scale, bank=bank: e.scalar_tensor_tensor(
                        xr[:, tt, :], psum[bank][:, 0:D], scale, xr[:, tt, :], ALU.mult, ALU.add), tk, share_done,
                        x_done)
                hid_free[hb] = tk
            w_free[i] = [tk]
            load_expert(n + 2)
        result = Slot(sem("result"))
        done = result.dma(sp, out.rearrange("b t d -> (b t) d").rearrange("(n p) d -> p n d", p=P), xr[:, :, :], y_done)
        sp.wait(done)


def kernel(x, ctx_1024, L0_attn_Wr, L0_attn_Wk, L0_attn_Wv, L0_attn_Ww, L0_attn_Wo, L0_ffn_gate_w,
           L0_ffn_w1, L0_ffn_w2, L0_ffn_w3, L0_ffn_sw1, L0_ffn_sw2, L0_ffn_sw3):
    import concourse.bacc as bacc
    from concourse.bass_utils import run_bass_kernel_spmd as run

    experts = lambda w, s: np.concatenate([np.asarray(w), np.asarray(s)[None]], axis=0).transpose(0, 2, 1)
    arrays = dict(
        x=x, ctx_nat=ctx_1024, ctx_tr=np.asarray(ctx_1024).transpose(0, 2, 1),
        wr_t=np.asarray(L0_attn_Wr).T, wk=L0_attn_Wk, wv_t=np.asarray(L0_attn_Wv).T, ww_t=np.asarray(L0_attn_Ww).T,
        wo_t=np.asarray(L0_attn_Wo).T, gate_t=np.asarray(L0_ffn_gate_w).T,
        w1_t=experts(L0_ffn_w1, L0_ffn_sw1), w3_t=experts(L0_ffn_w3, L0_ffn_sw3), w2_t=experts(L0_ffn_w2, L0_ffn_sw2))
    arrays = {f"{n}_dram": np.ascontiguousarray(a) for n, a in arrays.items()}
    nc = bacc.Bacc("TRN2", target_bir_lowering=False, num_devices=1)
    aps = [nc.dram_tensor(n, a.shape, mybir.dt.from_np(a.dtype), kind="ExternalInput").ap() for n, a in arrays.items()]
    result = nc.dram_tensor("out_dram", (B, T, D), F32, kind="ExternalOutput").ap()
    build(nc, *aps, result)
    return run(nc, [arrays], core_ids=[0]).results[0]["out_dram"]
```

```python
from contextlib import ExitStack

import numpy as np
import concourse.bass as bass
from concourse import mybir

F32 = mybir.dt.float32
I32 = mybir.dt.int32
U32 = mybir.dt.uint32
ALU = mybir.AluOpType
ACT = mybir.ActivationFunctionType
AX = mybir.AxisListType

P = 128
B, T, D = 32, 64, 256
N = 1601
KC = D // P
TILES = B * T // P
SEGS = 8
L = -(-N // SEGS)
GB = P // SEGS
GROUPS = B // GB
STEPS = T + SEGS - 1
SLOTS = STEPS + 1
W = L + 1
BIG = 1e30
QC = 2 * L
QUARTERS = SEGS // 2
HC = 2 * QC
CT = -(-N // P)
HEADS, HD = 16, 16
CH = 512
CHUNKS = B * T // CH
CTILES = CH // P
E, HID = 8, 704
HH = HID // 2
HC3 = -(-HH // P)
CB = 4
MOE_TILES = 2 * TILES + E - 1
EPS_LN = 1e-5
EPS_RMS = float(np.finfo(np.float32).eps)
TIE = -2e-37
HALF_RSQRT_MAGIC = float(0x5F3759DF - 0x00800000)


class Tick:
    def __init__(self, sem, value):
        self.sem, self.value = sem, value


class Lane:
    def __init__(self, engine, sem):
        self.engine, self.sem, self.count, self.seen = engine, sem, 0, {}

    def wait(self, *ticks):
        for t in ticks:
            if t is not None and self.seen.get(t.sem.name, 0) < t.value:
                self.seen[t.sem.name] = t.value
                self.engine.wait_ge(t.sem, t.value)

    def do(self, op, *waits):
        self.wait(*waits)
        self.count += 1
        op(self.engine).then_inc(self.sem, 1)
        return Tick(self.sem, self.count)

    def more(self, op, *waits):
        self.wait(*waits)
        op(self.engine)


class Slot:
    def __init__(self, sem):
        self.sem, self.count = sem, 0

    def dma(self, lane, out, in_, *waits):
        lane.wait(*waits)
        self.count += 16
        lane.engine.dma_start(out, in_).then_inc(self.sem, 16)
        return Tick(self.sem, self.count)


def bc(ap, n, at):
    ap = ap.unsqueeze(at)
    return ap.to_broadcast([n if k == at else s for k, s in enumerate(ap.shape)])


def interleave(main, other, each):
    for _ in main:
        for _ in range(each):
            next(other, None)
    run(other)


def together(*parts):
    parts = list(parts)
    while parts:
        for part in list(parts):
            try:
                next(part)
            except StopIteration:
                parts.remove(part)
        yield


def run(steps):
    for _ in steps:
        pass


def build(nc, x, ctx_nat, ctx_tr, wr_t, wk, wv_t, ww_t, wo_t, gate_t, w1_t, w3_t, w2_t, out):
    stack = ExitStack()
    with stack:
        sem = lambda name: stack.enter_context(nc.semaphore(name))
        psum = [stack.enter_context(nc.psum_tensor(f"bank{i}", [P, 512], F32)) for i in range(8)]
        pe, dve, act, pool, sp = (Lane(engine, sem(f"{n}_done")) for engine, n in (
            (nc.tensor, "pe"), (nc.vector, "dve"), (nc.scalar, "act"), (nc.gpsimd, "pool"), (nc.sync, "sp")))
        everyone = lambda: [Tick(l.sem, l.count) for l in (pe, dve, act, pool)]

        latents2 = nc.dram_tensor("latents2", (B * T, D), F32).ap()
        sorted_in = nc.dram_tensor("sorted_in", (MOE_TILES * P, D), F32).ap()
        sorted_out = nc.dram_tensor("sorted_out", (MOE_TILES * P, D), F32).ap()

        cursor = [nc.sbuf_base + (-nc.sbuf_base) % 32]

        def place(name, free, dt=F32):
            size = int(np.prod(free)) * 4
            at = cursor[0]
            cursor[0] += size + (-size) % 32
            assert cursor[0] <= nc.sbuf_usable_end, (name, cursor[0], nc.sbuf_usable_end)
            return nc.alloc_sbuf_tensor_at(name, [P] + list(free), dt, offset=at)

        def zone(size):
            at = cursor[0]
            cursor[0] += size + (-size) % 32
            return at

        ident = place("ident", [P])
        ones = place("ones", [P])
        before = place("before", [P])
        blocks = place("blocks", [P])
        row1 = place("row1", [L])
        rowP = place("rowP", [CT])
        lane_i = place("lane_i", [1], I32)
        seg_i = place("seg_i", [1], I32)
        seg, shift_rows, tiny = place("seg", [1]), place("shift_rows", [1]), place("tiny", [1])
        first_big = place("first_big", [1])
        start = place("start", [1])
        not_last = place("not_last", [1])
        inject = place("inject", [STEPS])
        expert_io = place("expert_io", [E])
        bb = place("bb", [TILES])
        threshold = [place(f"threshold{g}", [SLOTS]) for g in range(GROUPS)]
        stats = place("stats", [4, 6])
        mv = place("mv", [TILES, 2])
        ln_a, ln_b, ln_c, ln_d = (place(f"ln_{c}", [TILES]) for c in "abcd")
        shifted, reach = place("shifted", [1]), place("reach", [1])
        rms, rms2 = place("rms", [CTILES]), place("rms2", [CTILES])
        lg, sc, top8 = place("lg", [CTILES, E]), place("sc", [CTILES, E]), place("top8", [CTILES, 8])
        idx, ssum, den = place("idx", [CTILES, 8], U32), place("ssum", [CTILES]), place("den", [CTILES])
        idxf = place("idxf", [CTILES, 2])
        weight = place("weight", [TILES, 2])
        chosen = place("chosen", [2, TILES, E])
        slot_f, slot_i = place("slot_f", [TILES, 2]), place("slot_i", [TILES, 2], U32)
        tile_expert = place("tile_expert", [MOE_TILES], I32)

        lat_at = zone(TILES * D * 4)
        TABLE = SLOTS * W * 4
        PATH = -(-(3 * CT * D + 3 * CT * T + 2 * (T + 1) + 16) * 4 // 32) * 32
        HALF_TILES = 2 * (2 * HH + HC3 * P) * 4
        table_at = [zone(max(TABLE, PATH + HALF_TILES)), zone(TABLE)]
        work_at = cursor[0]
        W_UP, W_DN = 2 * KC * HID * 4, 2 * HC3 * D * 4
        end_at = nc.sbuf_usable_end // 32 * 32
        kept_at = end_at - (W_UP + W_DN + 2 * KC * CH * 4)

        def at(offset):
            cursor[0] = offset

        at(lat_at)
        latT = place("latT", [KC, B * T])
        table = []
        for g in range(GROUPS):
            at(table_at[g])
            table.append(place(f"table{g}", [SLOTS, W]))

        at(table_at[1])
        lat, latn = place("lat", [TILES, D]), place("latn", [TILES, D])
        zeros = place("zeros", [D])

        at(work_at)
        col_min = [place(f"col_min{i}", [CB, L]) for i in range(2)]
        above = place("above", [CB, L])
        across = place("across", [CB, L])
        best = place("best", [L])
        align_end = cursor[0]
        ctxT = [place(f"ctxT{i}", [2, KC, HC]) for i in range(2)]
        sq = [place(f"sq{i}", [2, KC, QC]) for i in range(2)]
        sqs = [place(f"sqs{i}", [2, QC]) for i in range(2)]
        z = [place(f"z{i}", [QC]) for i in range(2)]
        root = [place(f"root{i}", [QC]) for i in range(2)]
        root2 = place("root2", [QC])
        slope = place("slope", [QC])
        dist = [place(f"dist{i}", [QC]) for i in range(2)]

        at(table_at[0])
        rows_c = [place(f"rows_c{i}", [CT, D]) for i in range(3)]
        on_path = [place(f"on_path{i}", [CT, T]) for i in range(2)]
        below = place("below", [CT, T])
        cuts = [place(f"cuts{i}", [T + 1]) for i in range(2)]
        assert cursor[0] <= table_at[0] + PATH
        at(table_at[0] + PATH)
        act_s = [place(f"act_s{i}", [HH]) for i in range(2)]
        hid = [place(f"hid{i}", [HH]) for i in range(2)]
        hidT = [place(f"hidT{i}", [HC3, P]) for i in range(2)]

        at(lat_at)
        xr = place("xr", [TILES, D])

        at(align_end)
        w_r, w_v, w_w, w_o, w_ks = (place(n, [KC, D]) for n in ("w_r", "w_v", "w_w", "w_o", "w_ks"))
        w_g = place("w_g", [KC, E])
        hT = place("hT", [KC, CH])
        gate_at = cursor[0]
        gate_r, decay, kv, val = (place(n, [KC, CH]) for n in ("gate_r", "decay", "kv", "val"))
        assert cursor[0] <= kept_at, (cursor[0], kept_at)
        mix, mix2 = kv, val
        at(cursor[0] - KC * CH * 4)
        hn = place("hn", [CTILES, D])
        at(gate_at)
        w_k = place("w_k", [KC, D])
        at(kept_at)
        ws_up, ws_dn = place("ws_up", [2, KC, HID]), place("ws_dn", [2 * HC3, D])
        h2T = [place(f"h2T{i}", [KC, CH]) for i in range(2)]

        at(table_at[0])
        w_dn = place("w_dn", [E, 2 * HC3, D])
        assert cursor[0] <= table_at[0] + PATH
        at(table_at[1])
        w_up = place("w_up", [E, 2, KC, HID])
        moe_at = cursor[0]
        src = [place(f"src{i}", [D]) for i in range(3)]
        srcT = [place(f"srcT{i}", [KC, P]) for i in range(2)]
        y_sb = [place(f"y_sb{i}", [D]) for i in range(2)]
        back = [place(f"back{i}", [D]) for i in range((kept_at - cursor[0]) // (D * 4))]
        at(moe_at - TILES * D * 4)
        h2n = place("h2n", [TILES, D])
        h2n_at = moe_at - TILES * D * 4
        at(moe_at)
        tot_e, incl, base = place("tot_e", [E, TILES]), place("incl", [E, TILES]), place("base", [TILES, E])
        reset, prod = place("reset", [E, TILES]), place("prod", [TILES, E])
        tiles_i, tiles_f, tiles_cum = place("tiles_i", [E], I32), place("tiles_f", [E]), place("tiles_cum", [E])
        tile_io, cmp = place("tile_io", [MOE_TILES]), place("cmp", [MOE_TILES, E])

        c0 = pool.do(lambda e: e.memset(ident[:, :], 0.0))
        c_ident = pool.do(lambda e: e.affine_select(out=ident[:, :], in_=ident[:, :], compare_op=ALU.not_equal, fill=1.0,
                                                    base=0, pattern=[[-1, P]], channel_multiplier=1), c0)
        c_lane = pool.do(lambda e: e.iota(lane_i[:, :], [[0, 1]], base=0, channel_multiplier=1))
        iota = lambda tile_, pattern, base, step: pool.do(lambda e: e.iota(
            tile_, pattern, base=base, channel_multiplier=step, allow_small_or_imprecise_dtypes=True))
        c_rowP = iota(rowP[:, :], [[P, CT]], 1, 1)
        c_row = iota(row1[:, :], [[1, L]], 1, 0)
        c_step = iota(inject[:, :], [[1, STEPS]], 0, 0)
        c_expert = iota(expert_io[:, :], [[1, E]], 0, 0)
        c_b0 = pool.do(lambda e: e.memset(blocks[:, :], 1.0))
        heads_view = blocks[:, :].rearrange("p (h c) -> p h c", c=HD)
        c_b1 = pool.do(lambda e: e.affine_select(out=heads_view, in_=heads_view, compare_op=ALU.is_ge, fill=0.0, base=0,
                                                 pattern=[[-HD, P // HD], [0, HD]], channel_multiplier=1), c_b0)
        c_blocks = pool.do(lambda e: e.affine_select(out=heads_view, in_=heads_view, compare_op=ALU.is_ge, fill=0.0,
                                                     base=HD - 1, pattern=[[HD, P // HD], [0, HD]],
                                                     channel_multiplier=-1), c_b1)
        c_t0 = pool.do(lambda e: e.memset(before[:, :], 1.0))
        c_before = pool.do(lambda e: e.affine_select(out=before[:, :], in_=before[:, :], compare_op=ALU.is_gt, fill=0.0,
                                                     base=0, pattern=[[1, P]], channel_multiplier=-1), c_t0)
        c_zeros = pool.do(lambda e: e.memset(zeros[:, :], 0.0))
        c_ones = dve.do(lambda e: e.memset(ones[:, :], 1.0))
        c_tiny = dve.do(lambda e: e.memset(tiny[:, :], 1e-30))
        t0 = dve.do(lambda e: e.tensor_single_scalar(seg_i[:, :], lane_i[:, :], SEGS - 1, ALU.bitwise_and), c_lane)
        c_seg = dve.do(lambda e: e.tensor_copy(seg[:, :], seg_i[:, :]), t0)
        c_first = dve.do(lambda e: e.tensor_scalar(first_big[:, :], seg[:, :], 0.0, BIG, ALU.is_equal, ALU.mult), c_seg)
        c_start = dve.do(lambda e: e.tensor_scalar(start[:, :], seg[:, :], 0.0, BIG, ALU.is_gt, ALU.mult), c_seg)
        c_nlast = dve.do(lambda e: e.tensor_single_scalar(not_last[:, :], seg[:, :], float(SEGS - 1), ALU.is_lt), c_seg)
        t1 = dve.do(lambda e: e.tensor_scalar(shift_rows[:, :], seg[:, :], float(L), None, ALU.mult), c_seg)
        c_row1 = dve.do(lambda e: e.tensor_scalar(row1[:, :], row1[:, :], shift_rows[:, 0:1], None, ALU.add), t1, c_row)
        t2 = dve.do(lambda e: e.tensor_scalar(inject[:, :], inject[:, :], seg[:, 0:1], None, ALU.subtract), c_seg, c_step)
        c_inject = dve.do(lambda e: e.tensor_scalar(inject[:, :], inject[:, :], float(T), float(N), ALU.is_ge, ALU.mult), t2)

        bank_free = [None] * 8

        def layer_norm(src_, dst, n, *ready):
            for t in range(n):
                s = dve.do(lambda e: e.bn_stats(stats[:, t % 4, :], src_[:, t, :]), *ready)
                last = dve.do(lambda e: e.bn_aggr(mv[:, t, :], stats[:, t % 4, :]), s)
            v, r, a, c, d = mv[:, 0:n, 1], ln_a[:, 0:n], ln_b[:, 0:n], ln_c[:, 0:n], ln_d[:, 0:n]
            k = dve.do(lambda e: e.tensor_scalar(a, v, EPS_LN, None, ALU.add), last)
            k1 = act.do(lambda e: e.activation(r, a, ACT.Sqrt), k)
            k2 = dve.do(lambda e: e.reciprocal(c, r), k1)
            k3 = dve.do(lambda e: e.tensor_tensor(d, r, r, ALU.mult), k1)
            k4 = dve.do(lambda e: e.tensor_tensor(d, a, d, ALU.subtract), k3)
            k5 = dve.do(lambda e: e.scalar_tensor_tensor(d, d, 0.5, c, ALU.mult, ALU.mult), k4, k2)
            k6 = dve.do(lambda e: e.tensor_tensor(r, r, d, ALU.add), k5)
            k7 = dve.do(lambda e: e.reciprocal(c, r), k6)
            dve.wait(k7)
            for t in range(n):
                last = dve.do(lambda e: e.tensor_scalar(dst[:, t, :], src_[:, t, :], mv[:, t, 0:1], ln_c[:, t:t + 1],
                                                        ALU.subtract, ALU.mult))
            return last

        def transpose_pair(src_, t, dst, scale, bank, *ready):
            pe.wait(bank_free[bank], c_ident, *ready)
            for k in range(KC):
                for j in range(2):
                    tick = pe.do(lambda e: e.transpose(psum[bank][:, (2 * k + j) * P:(2 * k + j + 1) * P],
                                                       src_[:, t + j, k * P:(k + 1) * P], ident[:, :]))
            bank_free[bank] = act.do(lambda e: e.activation(dst, psum[bank][:, :].rearrange("p (k n) -> p k n", k=KC),
                                                            ACT.Copy, scale=scale), tick, *ready)
            return bank_free[bank]

        x_tiles = x.rearrange("b t d -> (b t) d").rearrange("(n p) d -> p n d", p=P)
        lat_in = Slot(sem("lat_in"))
        got_lat = lat_in.dma(sp, lat[:, :, :], x_tiles)
        clear_sorted = Slot(sem("clear_sorted"))
        sorted_clear = clear_sorted.dma(sp, sorted_in.rearrange("(k p) d -> p k d", p=P), bc(zeros[:, :], MOE_TILES, 1),
                                        c_zeros)
        lat_done = layer_norm(lat, latn, TILES, got_lat)
        for t in range(TILES):
            norm_sq = act.do(lambda e: e.activation(lat[:, t, :], latn[:, t, :], ACT.Square,
                                                    accum_out=bb[:, t:t + 1]), lat_done)
        for t in range(0, TILES, 2):
            latT_done = transpose_pair(latn, t, latT[:, :, t * P:(t + 2) * P], -2.0, t // 2 % 2, lat_done)
        prologue_done = [norm_sq, latT_done, lat_done]

        ctxT_in = [Slot(sem(f"ctxT_in{i}")) for i in range(2)]
        ctxT_free, ctxT_got = [[], []], {}
        dist_out = [Slot(sem(f"dist_out{i}")) for i in range(2)]
        dist_sent = [None, None]
        sq_free, sqs_free, z_free, root_free = [None, None], [None, None], [None, None], [None, None]
        single = dict(root2=None, slope=None)
        table_ready = {}

        def load_ctxT(n):
            if n >= 2 * TILES:
                return
            pair, half = divmod(n, 2)
            c0, c1 = half * HC, min(N, (half + 1) * HC)
            for b in range(2):
                ctxT_got[n] = ctxT_in[n % 2].dma(
                    sp, ctxT[n % 2][:, b, :, 0:c1 - c0],
                    ctx_tr[2 * pair + b].rearrange("(k p) i -> p k i", p=P)[:, :, c0:c1], *ctxT_free[n % 2])

        def clear_table(g, *ready):
            tb = table[g]
            pool.do(lambda e: e.memset(tb[:, 0:SEGS, :], BIG), *ready)
            pool.do(lambda e: e.memset(tb[:, T + 1:SLOTS, :], BIG))
            pool.do(lambda e: e.memset(tb[:, SEGS:T + 1, 1 + N - (SEGS - 1) * L:W], BIG))
            return pool.do(lambda e: e.memset(tb[:, SEGS:T + 1, 0:1], BIG))

        def unit_rows(u):
            return min(N, (u % QUARTERS + 1) * QC) - u % QUARTERS * QC

        def squares(u):
            n, q = divmod(u, 2)
            nq, i = unit_rows(u), u % 2
            s = act.do(lambda e: e.activation(sq[i][:, :, :, 0:nq], ctxT[n % 2][:, :, :, q * QC:q * QC + nq], ACT.Square),
                       ctxT_got[n], sq_free[i])
            added_ = pool.do(lambda e: e.tensor_tensor(sqs[i][:, :, 0:nq], sq[i][:, :, 0, 0:nq], sq[i][:, :, 1, 0:nq],
                                                       ALU.add), s, sqs_free[i])
            sq_free[i] = added_
            return s, added_

        def distance_unit(u, sq_ticks, cleared, dve_busy):
            n, half = divmod(u, 2)
            pair, q = divmod(u, QUARTERS)
            nq, i, bank = unit_rows(u), u % 2, u % 3
            ps = psum[bank]
            pe.wait(ctxT_got[n], bank_free[bank], *prologue_done, c_ones)
            for k in range(KC):
                for b in range(2):
                    read_ctxT = pe.do(lambda e: e.matmul(
                        ps[b * T:(b + 1) * T, 0:nq], latT[:, k, pair * P + b * T:pair * P + (b + 1) * T],
                        ctxT[n % 2][:, b, k, half * QC:half * QC + nq], start=(k == 0), stop=False))
            for b in range(2):
                tick = pe.do(lambda e: e.matmul(ps[b * T:(b + 1) * T, 0:nq], ones[:, 0:T], sqs[i][:, b, 0:nq],
                                                start=False, stop=True), sq_ticks[1])
            sqs_free[i] = tick
            ctxT_free[n % 2] = [read_ctxT, sq_ticks[0]]
            if half:
                load_ctxT(n + 2)
            zi, ri, r2, di, sl = z[i][:, 0:nq], root[i][:, 0:nq], root2[:, 0:nq], dist[i][:, 0:nq], slope[:, 0:nq]
            if dve_busy:
                z_done = act.do(lambda e: e.activation(zi, ps[:, 0:nq], ACT.Relu, bias=bb[:, pair:pair + 1]), tick, z_free[i])
            else:
                z_done = dve.do(lambda e: e.tensor_scalar(zi, ps[:, 0:nq], bb[:, pair:pair + 1], 0.0, ALU.add, ALU.max),
                                tick, z_free[i])
            bank_free[bank] = z_done
            root_done = act.do(lambda e: e.activation(ri, zi, ACT.Sqrt, bias=tiny[:, 0:1]), z_done, root_free[i], c_tiny)
            sq_done = act.do(lambda e: e.activation(r2, ri, ACT.Square), root_done, single["root2"])
            slope_done = dve.do(lambda e: e.tensor_scalar(sl.bitcast(I32), zi.bitcast(I32), -0.5, HALF_RSQRT_MAGIC,
                                                          ALU.mult, ALU.add), z_done, single["slope"])
            err = dve.do(lambda e: e.tensor_tensor(zi, zi, r2, ALU.subtract), sq_done, slope_done)
            single["root2"] = err
            corr = dve.do(lambda e: e.tensor_tensor(zi, zi, sl, ALU.mult), err)
            single["slope"] = corr
            done = (pool if dve_busy else dve).do(lambda e: e.tensor_tensor(di, ri, zi, ALU.add), corr, dist_sent[i])
            z_free[i] = root_free[i] = done
            g = pair * 2 // GB
            for b in range(2):
                for s in range(2):
                    m = min(L, nq - s * L)
                    sg = 2 * q + s
                    part = (2 * pair + b) % GB * SEGS + sg
                    dist_sent[i] = dist_out[i].dma(
                        sp, table[g][part:part + 1, 1 + sg:1 + sg + T, 1:1 + m],
                        dist[i][b * T:(b + 1) * T, s * L:s * L + m], done, cleared)

        def distances(g, cleared, dve_busy):
            per = QUARTERS * TILES // GROUPS
            units = range(g * per, (g + 1) * per)
            sq_ticks = squares(units[0])
            for u in units:
                ready = u + 1 in units and (u + 1) // 2 in ctxT_got
                ahead = squares(u + 1) if ready else None
                distance_unit(u, sq_ticks, cleared, dve_busy)
                if u + 1 in units:
                    sq_ticks = ahead or squares(u + 1)
                yield
            table_ready[g] = list(dist_sent)

        down = [31] + list(range(31))
        upwards = list(range(1, 32)) + [0]
        shift_free, code_free, min_free = [None], [None], [None, None]
        path_ready = {}

        def align(g):
            tb = table[g]
            dve.wait(*table_ready[g], c_first, c_start, c_row1, c_inject, c_nlast)
            pool.wait(*table_ready[g])

            def codes(k0, n, ready):
                mins = col_min[k0 // CB % 2][:, 0:n, :]
                left, diag, up = tb[:, k0:k0 + n, 1:W], tb[:, k0:k0 + n, 0:L], tb[:, k0 + 1:k0 + n + 1, 0:L]
                a, c = above[:, 0:n, :], across[:, 0:n, :]
                side = pool.do(lambda e: e.tensor_tensor(c, left, diag, ALU.subtract), *ready, code_free[0])
                gain = pool.do(lambda e: e.tensor_tensor(a, up, mins, ALU.subtract))
                min_free[k0 // CB % 2] = gain
                yield
                half = dve.do(lambda e: e.tensor_scalar(c, c, 0.0, -0.5, ALU.is_ge, ALU.mult), side)
                yield
                tied = dve.do(lambda e: e.scalar_tensor_tensor(a, c, TIE, a, ALU.mult, ALU.add), half, gain)
                rc = pool.do(lambda e: e.tensor_tensor(c, bc(row1[:, :], n, 1), c, ALU.add), tied)
                yield
                yield
                code_free[0] = dve.do(lambda e: e.scalar_tensor_tensor(left, a, 0.0, c, ALU.is_gt, ALU.mult), rc)

            halo = scan_done = None
            filler = iter(())
            for step in range(STEPS):
                prev, cur = tb[:, step, :], tb[:, step + 1, :]
                cm = col_min[step // CB % 2][:, step % CB, :]
                m = dve.do(lambda e: e.tensor_tensor(cm, prev[:, 1:W], prev[:, 0:L], ALU.min), halo, scan_done,
                           min_free[step // CB % 2])
                next(filler, None)
                first = start[:, 0:1] if step == 0 else cur[:, 0:1]
                scan_done = dve.do(lambda e: e.tensor_tensor_scan(cur[:, 1:W], cm, cur[:, 1:W], first, ALU.min, ALU.add), m)
                if step + 1 < STEPS:
                    nxt = tb[:, step + 2, :]
                    sh = dve.do(lambda e: e.stream_shuffle(shifted[:, 0:1], cur[:, L:W], down), scan_done, shift_free[0])
                    halo = shift_free[0] = dve.do(lambda e: e.tensor_scalar(nxt[:, 0:1], shifted[:, 0:1],
                                                                            first_big[:, 0:1], None, ALU.max), sh)
                if step % CB == CB - 1 or step == STEPS - 1:
                    for _ in filler:
                        pass
                    k0 = step // CB * CB
                    filler = codes(k0, step + 1 - k0, [scan_done, halo])
                    next(filler)
                yield
            for _ in filler:
                pass
            th = threshold[g]
            t_old = dve.do(lambda e: e.memset(th[:, STEPS:SLOTS], float(N)), code_free[0])
            for step in range(STEPS - 1, -1, -1):
                code, old, new = tb[:, step, 1:W], th[:, step + 1:step + 2], th[:, step:step + 1]
                a = dve.do(lambda e: e.scalar_tensor_tensor(best[:, :], row1[:, :], old, code, ALU.is_le, ALU.mult), t_old)
                s = dve.do(lambda e: e.stream_shuffle(shifted[:, 0:1], old, upwards), shift_free[0], t_old)
                r = dve.do(lambda e: e.tensor_reduce(reach[:, 0:1], best[:, :], AX.X, ALU.max), a)
                t_old = dve.do(lambda e: e.scalar_tensor_tensor(new, shifted[:, 0:1], not_last[:, 0:1], reach[:, 0:1],
                                                                ALU.mult, ALU.max), s, r)
                shift_free[0] = t_old
                if step >= T:
                    t_old = dve.do(lambda e: e.tensor_tensor(new, new, inject[:, step:step + 1], ALU.max), t_old)
                yield
            path_ready[g] = t_old

        cleared0 = clear_table(0)
        load_ctxT(0)
        load_ctxT(1)
        for _ in distances(0, cleared0, False):
            pass
        cleared1 = clear_table(1, sorted_clear, *prologue_done)
        interleave(distances(1, cleared1, True), align(0), 4)
        distances_done = everyone() + [t for t in dist_sent]
        table0_done = Tick(dve.sem, dve.count)

        x_in = Slot(sem("x_in"))
        got_x = x_in.dma(sp, xr[:, :, :], x_tiles, *distances_done)
        rows_in = [Slot(sem(f"rows_in{i}")) for i in range(3)]
        rows_free, rows_got = [[table0_done]] * 3, {}
        path_free, below_free, cuts_free = [table0_done] * 2, [table0_done], [table0_done] * 2
        added = {}

        def load_rows(b):
            if b >= B:
                return
            i = b % 3
            full = N // P * P
            rows_in[i].dma(sp, rows_c[i][:, 0:N // P, :], ctx_nat[b, 0:full, :].rearrange("(t p) d -> p t d", p=P),
                           *rows_free[i])
            rows_got[b] = rows_in[i].dma(sp, rows_c[i][0:N - full, N // P, :], ctx_nat[b, full:N, :])

        def path_mask(b):
            g, i, row = b // GB, b % 2, b % GB * SEGS
            tick = pe.do(lambda e: e.matmul(psum[2][:, 0:T + 1], ident[:, row:row + 1].to_broadcast([P, P]),
                                            threshold[g][:, 0:T + 1], start=True, stop=True), bank_free[2], path_ready[g])
            bank_free[2] = cut = act.do(lambda e: e.activation(cuts[i][:, :], psum[2][:, 0:T + 1], ACT.Copy), tick,
                                        cuts_free[i])
            rp, lo, hi = bc(rowP[:, :], T, 2), bc(cuts[i][:, 0:T], CT, 1), bc(cuts[i][:, 1:T + 1], CT, 1)
            a = dve.do(lambda e: e.tensor_tensor(on_path[i][:, :, :], rp, lo, ALU.is_ge), cut, path_free[i], c_rowP)
            h = dve.do(lambda e: e.tensor_tensor(below[:, :, :], rp, hi, ALU.is_le), below_free[0])
            cuts_free[i] = h
            below_free[0] = pool.do(lambda e: e.tensor_tensor(on_path[i][:, :, :], on_path[i][:, :, :], below[:, :, :],
                                                              ALU.mult), a, h)
            return below_free[0]

        def add_rows(pairs):
            for pair in pairs:
                masks = [path_mask(2 * pair), path_mask(2 * pair + 1)]
                bank = pair % 2
                pe.wait(bank_free[bank], *masks, rows_got[2 * pair], rows_got[2 * pair + 1])
                for t in range(CT):
                    k = min(P, N - t * P)
                    for b in range(2):
                        tick = pe.do(lambda e: e.matmul(psum[bank][b * T:(b + 1) * T, 0:D], on_path[b][0:k, t, :],
                                                        rows_c[(2 * pair + b) % 3][0:k, t, :], start=(t == 0),
                                                        stop=(t == CT - 1)))
                    if t == CT // 2:
                        yield
                path_free[0] = path_free[1] = tick
                for b in range(2):
                    rows_free[(2 * pair + b) % 3] = [tick]
                for b in range(2):
                    load_rows(2 * pair + b + 3)
                bank_free[bank] = added[pair] = dve.do(lambda e: e.tensor_tensor(
                    xr[:, pair, :], xr[:, pair, :], psum[bank][:, 0:D], ALU.add), tick, got_x)
                yield

        rec_in = Slot(sem("rec_in"))

        def load_recurrence():
            for tile_, source in ((w_k, wk), (w_r, wr_t), (w_v, wv_t), (w_w, ww_t), (w_o, wo_t), (w_g, gate_t)):
                got = rec_in.dma(sp, tile_[:, :, :], source.rearrange("(k p) n -> p k n", p=P), *distances_done)
            for k in range(KC):
                pe.wait(got, c_blocks, bank_free[3 + k])
                for oc in range(KC):
                    tick = pe.do(lambda e: e.matmul(psum[3 + k][:, oc * P:(oc + 1) * P], w_k[:, oc, k * P:(k + 1) * P],
                                                    blocks[:, :], start=True, stop=True))
                bank_free[3 + k] = act.do(lambda e: e.activation(w_ks[:, k, :], psum[3 + k][:, 0:D], ACT.Copy), tick, got)
            return bank_free[3 + KC - 1]

        latents2_out = Slot(sem("latents2_out"))
        chunk_end = {-1: []}
        h2T_ready, h2T_free = {}, [None, None]
        stored = [None]

        def recurrence(c):
            t0 = c * CTILES
            free = chunk_end[c - 1]
            y_done = layer_norm(xr[:, t0:t0 + CTILES, :], hn, CTILES, *(added[t] for t in range(t0, t0 + CTILES)),
                                *free, stored[0], *distances_done)
            yield
            for t in range(0, CTILES, 2):
                hT_done = transpose_pair(hn, t, hT[:, :, t * P:(t + 2) * P], 1.0, 3 + t // 2, y_done, *free)
            yield

            def project(w, oc, bank):
                pe.wait(bank_free[bank], hT_done, recurrence_ready)
                for k in range(KC):
                    tick = pe.do(lambda e: e.matmul(psum[bank][:, :], w[:, k, oc * P:(oc + 1) * P], hT[:, k, :],
                                                    start=(k == 0), stop=(k == KC - 1)))
                return tick

            for oc in range(KC):
                p = project(w_r, oc, 3)
                r_done = bank_free[3] = act.do(lambda e: e.activation(gate_r[:, oc, :], psum[3][:, :], ACT.Sigmoid), p)
                p = project(w_w, oc, 4)
                w_done = bank_free[4] = act.do(lambda e: e.activation(decay[:, oc, :], psum[4][:, :], ACT.Sigmoid), p)
                yield
                p = project(w_v, oc, 5)
                v_done = bank_free[5] = act.do(lambda e: e.activation(val[:, oc, :], psum[5][:, :], ACT.Copy), p)
                p = project(w_ks, oc, 2)
                w_done = dve.do(lambda e: e.tensor_scalar(decay[:, oc, :], decay[:, oc, :], 0.99, None, ALU.mult), w_done)
                w_done = dve.do(lambda e: e.memset(decay[:, oc, 0:CH:T], 0.0), w_done)
                kv_done = bank_free[2] = dve.do(lambda e: e.tensor_tensor(kv[:, oc, :], psum[2][:, :], val[:, oc, :],
                                                                          ALU.mult), p, v_done)
                yield
                s_done = dve.do(lambda e: e.tensor_tensor_scan(kv[:, oc, :], decay[:, oc, :], kv[:, oc, :], 0.0,
                                                               ALU.mult, ALU.add), w_done, kv_done)
                m_done = dve.do(lambda e: e.tensor_tensor(mix[:, oc, :], gate_r[:, oc, :], kv[:, oc, :], ALU.mult),
                                s_done, r_done)
                m2_done = act.do(lambda e: e.activation(mix2[:, oc, :], mix[:, oc, :], ACT.Square), m_done, kv_done)
                yield
            pe.wait(m2_done, bank_free[2])
            for t in range(CTILES):
                for k in range(KC):
                    tick = pe.do(lambda e: e.matmul(psum[2][:, t:t + 1], mix2[:, k, t * P:(t + 1) * P], ones[:, 0:1],
                                                    start=(k == 0), stop=(k == KC - 1)))
            squares_read = tick
            r1 = bank_free[2] = dve.do(lambda e: e.tensor_scalar(rms[:, :], psum[2][:, 0:CTILES], 1.0 / D, EPS_RMS,
                                                                 ALU.mult, ALU.add), tick)
            r2 = act.do(lambda e: e.activation(rms2[:, :], rms[:, :], ACT.Sqrt), r1)
            r3 = dve.do(lambda e: e.reciprocal(rms[:, :], rms2[:, :]), r2)
            yield
            for t in range(CTILES):
                bank = 4 + t % 2
                pe.wait(bank_free[bank], m_done)
                for k in range(KC):
                    tick = pe.do(lambda e: e.matmul(psum[bank][:, 0:D], mix[:, k, t * P:(t + 1) * P], w_o[:, k, :],
                                                    start=(k == 0), stop=(k == KC - 1)))
                x_done = bank_free[bank] = dve.do(lambda e: e.scalar_tensor_tensor(
                    xr[:, t0 + t, :], psum[bank][:, 0:D], rms[:, t:t + 1], xr[:, t0 + t, :], ALU.mult, ALU.add), tick, r3)
            mix_read = tick
            yield
            y_done = layer_norm(xr[:, t0:t0 + CTILES, :], hn, CTILES, x_done, squares_read)
            stored[0] = latents2_out.dma(sp, latents2.rearrange("(n p) d -> p n d", p=P)[:, t0:t0 + CTILES, :], hn[:, :, :],
                                         y_done)
            yield
            hb = h2T[c % 2]
            for t in range(0, CTILES, 2):
                h2_done = transpose_pair(hn, t, hb[:, :, t * P:(t + 2) * P], 1.0, 3 + t // 2, y_done, h2T_free[c % 2])
            h2T_ready[c] = h2_done
            pe.wait(h2_done, bank_free[2])
            for t in range(CTILES):
                for k in range(KC):
                    tick = pe.do(lambda e: e.matmul(psum[2][:, t * E:(t + 1) * E], hb[:, k, t * P:(t + 1) * P], w_g[:, k, :],
                                                    start=(k == 0), stop=(k == KC - 1)))
            yield
            g0 = bank_free[2] = dve.do(lambda e: e.tensor_copy(lg[:, :, :], psum[2][:, 0:CTILES * E].rearrange(
                "p (t e) -> p t e", e=E)), tick)
            g1 = dve.do(lambda e: e.tensor_reduce(ssum[:, :], lg[:, :, :], AX.X, ALU.max), g0)
            g2 = dve.do(lambda e: e.tensor_tensor(lg[:, :, :], lg[:, :, :], bc(ssum[:, :], E, 2), ALU.subtract), g1)
            g3 = act.do(lambda e: e.activation(sc[:, :, :], lg[:, :, :], ACT.Exp), g2)
            g4 = dve.do(lambda e: e.tensor_reduce(ssum[:, :], sc[:, :, :], AX.X, ALU.add), g3)
            g5 = dve.do(lambda e: e.reciprocal(ssum[:, :], ssum[:, :]), g4)
            g6 = dve.do(lambda e: e.tensor_tensor(sc[:, :, :], sc[:, :, :], bc(ssum[:, :], E, 2), ALU.mult), g5)
            yield
            for t in range(CTILES):
                g7 = dve.do(lambda e: e.max(top8[:, t, :], sc[:, t, :]), g6)
            for t in range(CTILES):
                g8 = dve.do(lambda e: e.max_index(idx[:, t, :], top8[:, t, :], sc[:, t, :]), g7)
            g9 = dve.do(lambda e: e.tensor_copy(idxf[:, :, :], idx[:, :, 0:2]), g8)
            g10 = dve.do(lambda e: e.scalar_tensor_tensor(den[:, :], top8[:, :, 0], 1e-20, top8[:, :, 1], ALU.add, ALU.add), g7)
            g11 = dve.do(lambda e: e.reciprocal(den[:, :], den[:, :]), g10)
            dve.do(lambda e: e.tensor_tensor(weight[:, t0:t0 + CTILES, :], top8[:, :, 0:2], bc(den[:, :], 2, 2), ALU.mult), g11)
            for k in range(2):
                gate_done = dve.do(lambda e: e.tensor_tensor(
                    chosen[:, k, t0:t0 + CTILES, :], bc(expert_io[:, :], CTILES, 1),
                    idxf[:, :, k:k + 1].to_broadcast([P, CTILES, E]), ALU.is_equal), g9, c_expert)
            chunk_end[c] = [mix_read, squares_read, gate_done, h2_done]
            yield

        w_in = {}
        src_in = [Slot(sem(f"src_in{i}")) for i in range(3)]
        y_out = [Slot(sem(f"y_out{i}")) for i in range(2)]
        src_free, srcT_free, y_sent = [None] * 3, [None, None], [None, None]
        act_free, hid_free, hidT_free = [None, None], [None, None], [None, None]
        loaded = {}
        last_shared = [None]
        counter = [0]

        def load_source(k):
            if k < MOE_TILES:
                loaded[k] = src_in[k % 3].dma(sp, src[k % 3][:, :], sorted_in[k * P:(k + 1) * P, :], *routed_ready,
                                              src_free[k % 3])

        def experts(units):
            state = {}

            def prepare(j):
                kind, t = units[j]
                if kind == "shared":
                    state[j] = dict(x=lambda k: h2T[t // CTILES % 2][:, k, t % CTILES * P:(t % CTILES + 1) * P],
                                    ready=[h2T_ready[t // CTILES], shared_ready],
                                    up=lambda m, k, c0: ws_up[:, m, k, c0:c0 + HH], dn=lambda r, c: ws_dn[0:r, c, :])
                    return
                i = t % 2
                pe.wait(loaded[t], bank_free[5], c_ident)
                for k in range(KC):
                    tick = pe.do(lambda e: e.transpose(psum[5][:, k * P:(k + 1) * P], src[t % 3][:, k * P:(k + 1) * P],
                                                       ident[:, :]))
                src_free[t % 3] = tick
                load_source(t + 3)
                bank_free[5] = act.do(lambda e: e.activation(srcT[i][:, :, :], psum[5][:, 0:D].rearrange(
                    "p (k n) -> p k n", k=KC), ACT.Copy), tick, srcT_free[i])
                pe.wait(experts_known)
                ex = pe.engine.value_load(tile_expert[0:1, t:t + 1], min_val=0, max_val=E - 1)
                state[j] = dict(x=lambda k: srcT[i][:, k, :], ready=[bank_free[5], *weights_ready],
                                up=lambda m, k, c0: w_up[:, bass.ds(ex, 1), m, k, c0:c0 + HH],
                                dn=lambda r, c: w_dn[0:r, bass.ds(ex, 1), c, :])

            def up(h):
                j, half = divmod(h, 2)
                s, i = state[j], h % 2
                for m in range(2):
                    bank = 2 * i + m
                    pe.wait(bank_free[bank], *s["ready"])
                    for k in range(KC):
                        tick = pe.do(lambda e: e.matmul(psum[bank][:, 0:HH], s["x"](k), s["up"](m, k, half * HH),
                                                        start=(k == 0), stop=(k == KC - 1)))
                    if m == 0:
                        bank_free[bank] = silu = act.do(lambda e: e.activation(act_s[i][:, :], psum[bank][:, 0:HH], ACT.Silu),
                                                        tick, act_free[i])
                if half:
                    if units[j][0] == "shared":
                        h2T_free[units[j][1] // CTILES % 2] = tick
                    else:
                        srcT_free[units[j][1] % 2] = tick
                bank_free[bank] = act_free[i] = s["hid"] = dve.do(lambda e: e.tensor_tensor(
                    hid[i][:, :], psum[bank][:, 0:HH], act_s[i][:, :], ALU.mult), tick, silu, hid_free[i])

            def turn(h):
                j, half = divmod(h, 2)
                s, i = state[j], h % 2
                pe.wait(bank_free[4], s["hid"])
                for c in range(HC3):
                    r = min(P, HH - c * P)
                    tick = pe.do(lambda e: e.transpose(psum[4][0:r, c * P:(c + 1) * P], hid[i][:, c * P:c * P + r], ident[:, :]))
                hid_free[i] = tick
                full = HH // P
                a = act.do(lambda e: e.activation(hidT[i][:, 0:full, :], psum[4][:, 0:full * P].rearrange(
                    "p (c n) -> p c n", c=full), ACT.Copy), tick, hidT_free[i])
                r = HH - full * P
                d = dve.do(lambda e: e.tensor_copy(hidT[i][0:r, full, :], psum[4][0:r, full * P:(full + 1) * P]), tick,
                           hidT_free[i], a)
                bank_free[4] = d
                s[("T", half)] = [a, d]

            def down_(h):
                j, half = divmod(h, 2)
                s, i = state[j], h % 2
                kind, t = units[j]
                bank = 6 + j % 2
                pe.wait(*s[("T", half)])
                if half == 0:
                    pe.wait(bank_free[bank])
                for c in range(HC3):
                    r = min(P, HH - c * P)
                    tick = pe.do(lambda e: e.matmul(psum[bank][:, 0:D], hidT[i][0:r, c, :], s["dn"](r, half * HC3 + c),
                                                    start=(half == 0 and c == 0), stop=(half == 1 and c == HC3 - 1)))
                hidT_free[i] = tick
                if half == 0:
                    return
                if kind == "shared":
                    bank_free[bank] = last_shared[0] = dve.do(lambda e: e.tensor_tensor(
                        xr[:, t, :], xr[:, t, :], psum[bank][:, 0:D], ALU.add), tick, *chunk_end[t // CTILES])
                else:
                    y = t % 2
                    bank_free[bank] = done_ = dve.do(lambda e: e.tensor_copy(y_sb[y][:, :], psum[bank][:, 0:D]), tick,
                                                     y_sent[y], *routed_ready)
                    y_sent[y] = y_out[y].dma(sp, sorted_out[t * P:(t + 1) * P, :], y_sb[y][:, :], done_)
                del state[j]

            n = 2 * len(units)
            prepare(0)
            for h in range(n + 2):
                if h < n:
                    up(h)
                if h % 2 == 0 and h // 2 + 1 < len(units):
                    prepare(h // 2 + 1)
                if 0 <= h - 1 < n:
                    turn(h - 1)
                if 0 <= h - 2 < n:
                    down_(h - 2)
                yield

        def load_weights(slot, up_tile, dn_tile, n, *ready, parts=("up", "dn")):
            if "up" in parts:
                for m, source in enumerate((w1_t, w3_t)):
                    tick = slot.dma(sp, up_tile[:, m, :, :], source[n].rearrange("(k p) n -> p k n", p=P), *ready)
            if "dn" in parts:
                full = HH // P
                for half in range(2):
                    r0 = half * HH
                    slot.dma(sp, dn_tile[:, half * HC3:half * HC3 + full, :],
                             w2_t[n, r0:r0 + full * P, :].rearrange("(k p) n -> p k n", p=P), *ready)
                    tick = slot.dma(sp, dn_tile[0:HH - full * P, half * HC3 + full, :], w2_t[n, r0 + full * P:r0 + HH, :])
            return tick

        for b in range(3):
            load_rows(b)
        recurrence_ready = load_recurrence()
        shared_ready = load_weights(Slot(sem("shared_in")), ws_up, ws_dn, E, *distances_done)
        shared_tiles = lambda c: experts([("shared", t) for t in range(c * CTILES, (c + 1) * CTILES)])

        def behind_first():
            yield from add_rows(range(0, 4))
            yield from together(recurrence(0), add_rows(range(4, 8)))
            yield from together(recurrence(1), shared_tiles(0))
            yield from shared_tiles(1)

        interleave(align(1), behind_first(), 1)
        table1_done = Tick(dve.sem, dve.count)
        up_in, dn_in = Slot(sem("up_in")), Slot(sem("dn_in"))
        early = (align_end - table_at[1]) // W_UP
        for n in range(early):
            load_weights(up_in, w_up[:, n], None, n, table1_done, parts=("up",))
        run(add_rows(range(8, 12)))
        run(together(recurrence(2), add_rows(range(12, 16))))
        path_done = everyone()
        for n in range(E):
            dn_got = load_weights(dn_in, None, w_dn[:, n], n, *path_done, parts=("dn",))
        run(together(recurrence(3), shared_tiles(2)))

        rec_done = everyone()
        reload = Slot(sem("reload"))
        h2n_got = reload.dma(sp, h2n[:, :, :], latents2.rearrange("(n p) d -> p n d", p=P), stored[0], *rec_done)
        c_reset = dve.do(lambda e: e.memset(reset[:, :, :], 1.0), *rec_done)
        c_reset = dve.do(lambda e: e.memset(reset[:, :, 0:1], 0.0), c_reset)
        c_tile = pool.do(lambda e: e.iota(tile_io[:, :], [[1, MOE_TILES]], base=0, channel_multiplier=0,
                                          allow_small_or_imprecise_dtypes=True), *rec_done)
        both = dve.do(lambda e: e.tensor_tensor(prod[:, :, :], chosen[:, 0, :, :], chosen[:, 1, :, :], ALU.add), *rec_done)
        flat = lambda tile_: tile_[:, :, :].rearrange("p t e -> p (t e)")
        pe.wait(bank_free[0], bank_free[1], c_before, both)
        pe.do(lambda e: e.matmul(psum[0][:, 0:TILES * E], before[:, :], flat(prod), start=True, stop=True))
        s0 = pe.do(lambda e: e.matmul(psum[1][:, 0:TILES * E], ones[:, :], flat(prod), start=True, stop=True))
        s1 = dve.do(lambda e: e.tensor_copy(tot_e[:, :, :], psum[1][:, 0:TILES * E].rearrange("p (t e) -> p e t", e=E)), s0)
        bank_free[1] = s1
        s2 = dve.do(lambda e: e.tensor_tensor_scan(incl[:, :, :].rearrange("p e t -> p (e t)"),
                                                   reset[:, :, :].rearrange("p e t -> p (e t)"),
                                                   tot_e[:, :, :].rearrange("p e t -> p (e t)"), 0.0, ALU.mult, ALU.add),
                    s1, c_reset)
        s3 = dve.do(lambda e: e.tensor_scalar(tiles_i[:, :], incl[:, :, TILES - 1], float(P - 1), None, ALU.add), s2)
        s4 = dve.do(lambda e: e.tensor_single_scalar(tiles_i[:, :], tiles_i[:, :], 7, ALU.logical_shift_right), s3)
        s5 = dve.do(lambda e: e.tensor_copy(tiles_f[:, :], tiles_i[:, :]), s4)
        s6 = dve.do(lambda e: e.tensor_tensor_scan(tiles_cum[:, :], ones[:, 0:E], tiles_f[:, :], 0.0, ALU.mult, ALU.add), s5)
        s7 = dve.do(lambda e: e.tensor_tensor(cmp[:, :, :], bc(tile_io[:, :], E, 2), bc(tiles_cum[:, :], MOE_TILES, 1),
                                              ALU.is_ge), s6, c_tile)
        s8 = dve.do(lambda e: e.tensor_reduce(tile_io[:, :], cmp[:, :, :], AX.X, ALU.add), s7)
        experts_known = dve.do(lambda e: e.tensor_scalar(tile_expert[:, :], tile_io[:, :], float(E - 1), None, ALU.min), s8)
        p0 = dve.do(lambda e: e.tensor_tensor(tiles_f[:, :], tiles_cum[:, :], tiles_f[:, :], ALU.subtract), s6)
        p1 = dve.do(lambda e: e.tensor_tensor(incl[:, :, :], incl[:, :, :], tot_e[:, :, :], ALU.subtract), s3)
        p2 = dve.do(lambda e: e.tensor_tensor(base[:, :, :], psum[0][:, 0:TILES * E].rearrange("p (t e) -> p t e", e=E),
                                              incl[:, :, :].rearrange("p e t -> p t e"), ALU.add), p1)
        bank_free[0] = p2
        p3 = dve.do(lambda e: e.scalar_tensor_tensor(base[:, :, :], bc(tiles_f[:, :], TILES, 1), float(P), base[:, :, :],
                                                     ALU.mult, ALU.add), p0, p2)
        for k in range(2):
            p4 = dve.do(lambda e: e.tensor_tensor(prod[:, :, :], chosen[:, k, :, :], base[:, :, :], ALU.mult), p3, s0)
            p3 = dve.do(lambda e: e.tensor_reduce(slot_f[:, :, k], prod[:, :, :], AX.X, ALU.add), p4)
        slots_known = dve.do(lambda e: e.tensor_copy(slot_i[:, :, :], slot_f[:, :, :]), p3)
        sort_out = Slot(sem("sort_out"))
        pool.wait(slots_known, h2n_got, sorted_clear)
        for t in range(TILES):
            for k in range(2):
                sort_out.count += 16
                pool.engine.indirect_dma_start(
                    out=sorted_in[:, :], out_offset=bass.IndirectOffsetOnAxis(ap=slot_i[:, t, k:k + 1], axis=0),
                    in_=h2n[:, t, :], in_offset=None).then_inc(sort_out.sem, 16)
        sorted_done = Tick(sort_out.sem, sort_out.count)
        routed_ready = [sorted_done, slots_known, experts_known]
        for n in range(early, E):
            up_got = load_weights(up_in, w_up[:, n], None, n, sorted_done, *rec_done, parts=("up",))
        weights_ready = [up_got, dn_got]
        for k in range(3):
            load_source(k)

        run(experts([("routed", k) for k in range(MOE_TILES)] + [("shared", t) for t in range(3 * CTILES, TILES)]))

        back_in = [Slot(sem(f"back_in{i}")) for i in range(len(back))]
        back_free = [None] * len(back)
        result = Slot(sem("result"))
        out_tiles = out.rearrange("b t d -> (b t) d").rearrange("(n p) d -> p n d", p=P)
        pool.wait(*y_sent)
        n = 0
        for t in range(TILES):
            for k in range(2):
                i = n % len(back)
                n += 1
                pool.wait(back_free[i], *routed_ready)
                back_in[i].count += 16
                pool.engine.indirect_dma_start(
                    out=back[i][:, :], out_offset=None, in_=sorted_out[:, :],
                    in_offset=bass.IndirectOffsetOnAxis(ap=slot_i[:, t, k:k + 1], axis=0)).then_inc(back_in[i].sem, 16)
                back_free[i] = done = dve.do(lambda e: e.scalar_tensor_tensor(
                    xr[:, t, :], back[i][:, :], weight[:, t, k:k + 1], xr[:, t, :], ALU.mult, ALU.add),
                    Tick(back_in[i].sem, back_in[i].count), last_shared[0], Tick(dve.sem, dve.count))
            if t % 4 == 3:
                end = result.dma(sp, out_tiles[:, t - 3:t + 1, :], xr[:, t - 3:t + 1, :], done)
        sp.wait(end)


def kernel(x, ctx_1024, L0_attn_Wr, L0_attn_Wk, L0_attn_Wv, L0_attn_Ww, L0_attn_Wo, L0_ffn_gate_w,
           L0_ffn_w1, L0_ffn_w2, L0_ffn_w3, L0_ffn_sw1, L0_ffn_sw2, L0_ffn_sw3):
    import concourse.bacc as bacc
    from concourse.bass_utils import run_bass_kernel_spmd as run

    experts = lambda w, s: np.concatenate([np.asarray(w), np.asarray(s)[None]], axis=0).transpose(0, 2, 1)
    arrays = dict(
        x=x, ctx_nat=ctx_1024, ctx_tr=np.asarray(ctx_1024).transpose(0, 2, 1),
        wr_t=np.asarray(L0_attn_Wr).T, wk=L0_attn_Wk, wv_t=np.asarray(L0_attn_Wv).T, ww_t=np.asarray(L0_attn_Ww).T,
        wo_t=np.asarray(L0_attn_Wo).T, gate_t=np.asarray(L0_ffn_gate_w).T,
        w1_t=experts(L0_ffn_w1, L0_ffn_sw1), w3_t=experts(L0_ffn_w3, L0_ffn_sw3), w2_t=experts(L0_ffn_w2, L0_ffn_sw2))
    arrays = {f"{n}_dram": np.ascontiguousarray(a) for n, a in arrays.items()}
    nc = bacc.Bacc("TRN2", target_bir_lowering=False, num_devices=1)
    aps = [nc.dram_tensor(n, a.shape, mybir.dt.from_np(a.dtype), kind="ExternalInput").ap() for n, a in arrays.items()]
    result = nc.dram_tensor("out_dram", (B, T, D), F32, kind="ExternalOutput").ap()
    build(nc, *aps, result)
    return run(nc, [arrays], core_ids=[0]).results[0]["out_dram"]
```

```python
from contextlib import ExitStack

import numpy as np
import concourse.bass as bass
from concourse import mybir

F32 = mybir.dt.float32
BF16 = mybir.dt.bfloat16
I32 = mybir.dt.int32
U32 = mybir.dt.uint32
ALU = mybir.AluOpType
ACT = mybir.ActivationFunctionType
AX = mybir.AxisListType

P = 128
B, T, D = 32, 64, 256
N = 1601
KC = D // P
TILES = B * T // P
SEGS = 8
L = -(-N // SEGS)
GB = P // SEGS
GROUPS = B // GB
STEPS = T + SEGS - 1
SLOTS = STEPS + 1
W = L + 1
BIG = 1e30
QC = 2 * L
QUARTERS = SEGS // 2
HC = 2 * QC
CT = -(-N // P)
CTH = -(-CT // 2)
ROWS_RING = 5
HD = 16
CH = 512
CHUNKS = B * T // CH
CTILES = CH // P
E, HID = 8, 704
HH = HID // 2
HC3 = -(-HH // P)
LAST = 4
LEAD = 2
CB = 4
MOE_TILES = 2 * TILES + E - 1
EPS_LN = 1e-5
EPS_RMS = float(np.finfo(np.float32).eps)
TIE = -4e-37
HALF_RSQRT_MAGIC = float(0x5F3759DF - 0x00800000)


class Tick:
    def __init__(self, sem, value):
        self.sem, self.value = sem, value


class Lane:
    def __init__(self, engine, sem):
        self.engine, self.sem, self.count, self.seen = engine, sem, 0, {}

    def wait(self, *ticks):
        for t in ticks:
            if t is not None and self.seen.get(t.sem.name, 0) < t.value:
                self.seen[t.sem.name] = t.value
                self.engine.wait_ge(t.sem, t.value)

    def do(self, op, *waits):
        self.wait(*waits)
        self.count += 1
        op(self.engine).then_inc(self.sem, 1)
        return Tick(self.sem, self.count)

    def more(self, op, *waits):
        self.wait(*waits)
        op(self.engine)


class Slot:
    def __init__(self, sem):
        self.sem, self.count = sem, 0

    def dma(self, lane, out, in_, *waits):
        lane.wait(*waits)
        self.count += 16
        lane.engine.dma_start(out, in_).then_inc(self.sem, 16)
        return Tick(self.sem, self.count)


def bc(ap, n, at):
    ap = ap.unsqueeze(at)
    return ap.to_broadcast([n if k == at else s for k, s in enumerate(ap.shape)])


def interleave(main, other, each):
    for n, _ in enumerate(main):
        for _ in range(each(n)):
            next(other, None)
    run(other)


def together(*parts):
    parts = list(parts)
    while parts:
        for part in list(parts):
            try:
                next(part)
            except StopIteration:
                parts.remove(part)
        yield


def run(steps):
    for _ in steps:
        pass


def build(nc, x, ctx_nat, ctx_tr, wr_t, wk, wv_t, ww_t, wo_t, gate_t, w1_t, w3_t, w2_t, out):
    stack = ExitStack()
    with stack:
        sem = lambda name: stack.enter_context(nc.semaphore(name))
        psum = [stack.enter_context(nc.psum_tensor(f"bank{i}", [P, 512], F32)) for i in range(8)]
        pe, dve, act, pool, sp = (Lane(engine, sem(f"{n}_done")) for engine, n in (
            (nc.tensor, "pe"), (nc.vector, "dve"), (nc.scalar, "act"), (nc.gpsimd, "pool"), (nc.sync, "sp")))
        everyone = lambda: [Tick(l.sem, l.count) for l in (pe, dve, act, pool)]

        latents2 = nc.dram_tensor("latents2", (B * T, D), F32).ap()
        sorted_out = nc.dram_tensor("sorted_out", (MOE_TILES * P, D), F32).ap()

        cursor = [nc.sbuf_base + (-nc.sbuf_base) % 32]

        def place(name, free, dt=F32):
            size = int(np.prod(free)) * mybir.dt.size(dt)
            at = cursor[0]
            cursor[0] += size + (-size) % 32
            assert cursor[0] <= nc.sbuf_usable_end, (name, cursor[0], nc.sbuf_usable_end)
            return nc.alloc_sbuf_tensor_at(name, [P] + list(free), dt, offset=at)

        def zone(size):
            at = cursor[0]
            cursor[0] += size + (-size) % 32
            return at

        ident = place("ident", [P])
        ones = place("ones", [P])
        before = place("before", [P])
        blocks = place("blocks", [P])
        row1 = place("row1", [L])
        row75 = place("row75", [L])
        rowP = place("rowP", [CT])
        lane_i = place("lane_i", [1], I32)
        seg_i = place("seg_i", [1], I32)
        seg, shift_rows, tiny = place("seg", [1]), place("shift_rows", [1]), place("tiny", [1])
        first_big = place("first_big", [1])
        start = place("start", [1])
        not_last = place("not_last", [1])
        inject = place("inject", [STEPS])
        expert_io = place("expert_io", [E])
        bb = place("bb", [TILES])
        threshold = [place(f"threshold{g}", [SLOTS]) for g in range(GROUPS)]
        stats = place("stats", [4, 6])
        mv = place("mv", [TILES, 2])
        ln_a, ln_b, ln_c, ln_d = (place(f"ln_{c}", [TILES]) for c in "abcd")
        shifted, reach = place("shifted", [1]), place("reach", [1])
        rms, rms2 = place("rms", [CTILES]), place("rms2", [CTILES])
        lg, sc, top8 = place("lg", [CTILES, E]), place("sc", [CTILES, E]), place("top8", [CTILES, 8])
        idx, ssum, den = place("idx", [CTILES, 8], U32), place("ssum", [CTILES]), place("den", [CTILES])
        idxf = place("idxf", [CTILES, 2])
        weight = place("weight", [TILES, 2])
        chosen = place("chosen", [2, TILES, E])
        slot_f, slot_i = place("slot_f", [TILES, 2]), place("slot_i", [TILES, 2], U32)
        tile_expert = place("tile_expert", [MOE_TILES], I32)
        order = place("order", [MOE_TILES], U32)

        lat_at = zone(TILES * D * 4)
        TABLE = SLOTS * W * 4
        PATH = -(-(ROWS_RING * CTH * D + 4 * CT * T + 2 * (T + 1) + 16) * 4 // 32) * 32
        HALF_TILES = 2 * (2 * HH + HC3 * P) * 4
        table_at = [zone(max(TABLE, PATH + HALF_TILES)), zone(TABLE)]
        work_at = cursor[0]
        W_UP, W_DN = 2 * KC * HID * 4, 2 * HC3 * D * 4
        end_at = nc.sbuf_usable_end // 32 * 32
        kept_at = end_at - (W_UP + W_DN + 2 * KC * CH * 4)

        def at(offset):
            cursor[0] = offset

        at(lat_at)
        latT = place("latT", [KC, B * T])
        table = []
        for g in range(GROUPS):
            at(table_at[g])
            table.append(place(f"table{g}", [SLOTS, W]))

        at(table_at[1])
        lat, latn = place("lat", [TILES, D]), [place(f"latn{i}", [CTILES, D]) for i in range(2)]
        more_ctxT = [place(f"ctxT{i}", [2, KC, HC]) for i in (2, 3)]
        assert cursor[0] <= table_at[1] + TABLE

        at(work_at)
        col_min = [place(f"col_min{i}", [CB, L]) for i in range(2)]
        above = [place(f"above{i}", [CB, L]) for i in range(2)]
        across = [place(f"across{i}", [CB, L]) for i in range(2)]
        align_end = cursor[0]
        ctxT = [place(f"ctxT{i}", [2, KC, HC]) for i in range(2)] + more_ctxT
        sq = [place(f"sq{i}", [2, KC, QC]) for i in range(2)]
        z = [place(f"z{i}", [QC]) for i in range(2)]
        root = [place(f"root{i}", [QC]) for i in range(2)]
        root2 = [place(f"root2{i}", [QC]) for i in range(2)]
        dist = [place(f"dist{i}", [QC]) for i in range(2)]

        at(table_at[0])
        rows_c = [place(f"rows_c{i}", [CTH, D]) for i in range(ROWS_RING)]
        on_path = [place(f"on_path{i}", [CT, T]) for i in range(3)]
        from_row, to_row = place("from_row", [CT, T], BF16), place("to_row", [CT, T], BF16)
        cuts = [place(f"cuts{i}", [T + 1]) for i in range(2)]
        assert cursor[0] <= table_at[0] + PATH
        at(table_at[0] + PATH)
        act_s = [place(f"act_s{i}", [HH]) for i in range(2)]
        hid = [place(f"hid{i}", [HH]) for i in range(2)]
        hidT = [place(f"hidT{i}", [HC3, P]) for i in range(2)]

        at(lat_at)
        xr = place("xr", [TILES, D])

        at(align_end)
        w_r, w_v, w_w, w_o, w_ks = (place(n, [KC, D]) for n in ("w_r", "w_v", "w_w", "w_o", "w_ks"))
        w_g = place("w_g", [KC, E])
        hT = place("hT", [KC, CH])
        gate_at = cursor[0]
        gate_r, decay = place("gate_r", [CH]), place("decay", [CH])
        kv, val = place("kv", [KC, CH]), place("val", [KC, CH])
        assert cursor[0] <= kept_at, (cursor[0], kept_at)
        mix, mix2 = kv, val
        at(cursor[0] - KC * CH * 4)
        hn = place("hn", [CTILES, D])
        at(gate_at)
        w_k = place("w_k", [KC, D])
        at(kept_at)
        ws_up, ws_dn = place("ws_up", [2, KC, HID]), place("ws_dn", [2 * HC3, D])
        h2T = [place(f"h2T{i}", [KC, CH]) for i in range(2)]

        at(table_at[0])
        w_dn = place("w_dn", [E, 2 * HC3, D])
        assert cursor[0] <= table_at[0] + PATH
        at(table_at[1])
        w_up = place("w_up", [E, 2, KC, HID])
        moe_at = cursor[0]
        src = [place(f"src{i}", [D]) for i in range(3)]
        srcT = [place(f"srcT{i}", [KC, P]) for i in range(2)]
        y_sb = [place(f"y_sb{i}", [D]) for i in range(2)]
        at(table_at[1])
        back = place("back", [TILES, 2, D])
        at(moe_at)
        tot_e, incl, base = place("tot_e", [E, TILES]), place("incl", [E, TILES]), place("base", [TILES, E])
        reset, prod = place("reset", [E, TILES]), place("prod", [TILES, E])
        tiles_i, tiles_f, tiles_cum = place("tiles_i", [E], I32), place("tiles_f", [E]), place("tiles_cum", [E])
        tile_io, cmp = place("tile_io", [MOE_TILES]), place("cmp", [MOE_TILES, E])
        tile_no, place_no, token_no = place("tile_no", [MOE_TILES]), place("place_no", [P]), place("token_no", [TILES])
        tile_of_i, place_of_i = place("tile_of_i", [TILES, 2], I32), place("place_of_i", [TILES, 2], I32)
        tile_of, place_of = place("tile_of", [TILES, 2]), place("place_of", [TILES, 2])
        at_place = [place(f"at_place{i}", [CTILES, P]) for i in range(2)]
        in_tile = [place(f"in_tile{i}", [CTILES, MOE_TILES]) for i in range(2)]
        assert cursor[0] <= kept_at

        c0 = pool.do(lambda e: e.memset(ident[:, :], 0.0))
        c_ident = pool.do(lambda e: e.affine_select(out=ident[:, :], in_=ident[:, :], compare_op=ALU.not_equal, fill=1.0,
                                                    base=0, pattern=[[-1, P]], channel_multiplier=1), c0)
        c_lane = pool.do(lambda e: e.iota(lane_i[:, :], [[0, 1]], base=0, channel_multiplier=1))
        iota = lambda tile_, pattern, base, step: pool.do(lambda e: e.iota(
            tile_, pattern, base=base, channel_multiplier=step, allow_small_or_imprecise_dtypes=True))
        c_rowP = iota(rowP[:, :], [[P, CT]], 1, 1)
        c_row = iota(row1[:, :], [[1, L]], 1, 0)
        c_step = iota(inject[:, :], [[1, STEPS]], 0, 0)
        c_expert = iota(expert_io[:, :], [[1, E]], 0, 0)
        c_b0 = pool.do(lambda e: e.memset(blocks[:, :], 1.0))
        heads_view = blocks[:, :].rearrange("p (h c) -> p h c", c=HD)
        c_b1 = pool.do(lambda e: e.affine_select(out=heads_view, in_=heads_view, compare_op=ALU.is_ge, fill=0.0, base=0,
                                                 pattern=[[-HD, P // HD], [0, HD]], channel_multiplier=1), c_b0)
        c_blocks = pool.do(lambda e: e.affine_select(out=heads_view, in_=heads_view, compare_op=ALU.is_ge, fill=0.0,
                                                     base=HD - 1, pattern=[[HD, P // HD], [0, HD]],
                                                     channel_multiplier=-1), c_b1)
        c_t0 = pool.do(lambda e: e.memset(before[:, :], 1.0))
        c_before = pool.do(lambda e: e.affine_select(out=before[:, :], in_=before[:, :], compare_op=ALU.is_gt, fill=0.0,
                                                     base=0, pattern=[[1, P]], channel_multiplier=-1), c_t0)
        c_ones = dve.do(lambda e: e.memset(ones[:, :], 1.0))
        c_tiny = dve.do(lambda e: e.memset(tiny[:, :], 1e-30))
        t0 = dve.do(lambda e: e.tensor_single_scalar(seg_i[:, :], lane_i[:, :], SEGS - 1, ALU.bitwise_and), c_lane)
        c_seg = dve.do(lambda e: e.tensor_copy(seg[:, :], seg_i[:, :]), t0)
        c_first = dve.do(lambda e: e.tensor_scalar(first_big[:, :], seg[:, :], 0.0, BIG, ALU.is_equal, ALU.mult), c_seg)
        c_start = dve.do(lambda e: e.tensor_scalar(start[:, :], seg[:, :], 0.0, BIG, ALU.is_gt, ALU.mult), c_seg)
        c_nlast = dve.do(lambda e: e.tensor_single_scalar(not_last[:, :], seg[:, :], float(SEGS - 1), ALU.is_lt), c_seg)
        t1 = dve.do(lambda e: e.tensor_scalar(shift_rows[:, :], seg[:, :], float(L), None, ALU.mult), c_seg)
        c_row1 = dve.do(lambda e: e.tensor_scalar(row1[:, :], row1[:, :], shift_rows[:, 0:1], None, ALU.add), t1, c_row)
        c_row75 = dve.do(lambda e: e.tensor_scalar(row75[:, :], row1[:, :], -0.25, None, ALU.add), c_row1)
        t2 = dve.do(lambda e: e.tensor_scalar(inject[:, :], inject[:, :], seg[:, 0:1], None, ALU.subtract), c_seg, c_step)
        c_inject = dve.do(lambda e: e.tensor_scalar(inject[:, :], inject[:, :], float(T), float(N), ALU.is_ge, ALU.mult), t2)

        bank_free = [None] * 8

        def layer_norm(src_, dst, n, *ready):
            for t in range(n):
                s = dve.do(lambda e: e.bn_stats(stats[:, t % 4, :], src_[:, t, :]), *ready)
                last = dve.do(lambda e: e.bn_aggr(mv[:, t, :], stats[:, t % 4, :]), s)
                if t % 2:
                    yield
            v, r, a, c, d = mv[:, 0:n, 1], ln_a[:, 0:n], ln_b[:, 0:n], ln_c[:, 0:n], ln_d[:, 0:n]
            k = dve.do(lambda e: e.tensor_scalar(a, v, EPS_LN, None, ALU.add), last)
            k1 = act.do(lambda e: e.activation(r, a, ACT.Sqrt), k)
            yield
            k2 = dve.do(lambda e: e.reciprocal(c, r), k1)
            k3 = dve.do(lambda e: e.tensor_tensor(d, r, r, ALU.mult), k1)
            k4 = dve.do(lambda e: e.tensor_tensor(d, a, d, ALU.subtract), k3)
            k5 = dve.do(lambda e: e.scalar_tensor_tensor(d, d, 0.5, c, ALU.mult, ALU.mult), k4, k2)
            k6 = dve.do(lambda e: e.tensor_tensor(r, r, d, ALU.add), k5)
            k7 = dve.do(lambda e: e.reciprocal(c, r), k6)
            yield
            dve.wait(k7)
            for t in range(n):
                last = dve.do(lambda e: e.tensor_scalar(dst[:, t, :], src_[:, t, :], mv[:, t, 0:1], ln_c[:, t:t + 1],
                                                        ALU.subtract, ALU.mult))
                if t % 2:
                    yield
            return last

        def transpose_pair(src_, t, dst, scale, bank, *ready):
            pe.wait(bank_free[bank], c_ident, *ready)
            for k in range(KC):
                for j in range(2):
                    tick = pe.do(lambda e: e.transpose(psum[bank][:, (2 * k + j) * P:(2 * k + j + 1) * P],
                                                       src_[:, t + j, k * P:(k + 1) * P], ident[:, :]))
            bank_free[bank] = act.do(lambda e: e.activation(dst, psum[bank][:, :].rearrange("p (k n) -> p k n", k=KC),
                                                            ACT.Copy, scale=scale), tick, *ready)
            return bank_free[bank]

        x_tiles = x.rearrange("b t d -> (b t) d").rearrange("(n p) d -> p n d", p=P)
        latents_ready = {}
        lat_got = {}

        def load_latents():
            for c in range(CHUNKS):
                lat_got[c] = Slot(sem(f"lat_in{c}")).dma(sp, lat[:, c * CTILES:(c + 1) * CTILES, :],
                                                         x_tiles[:, c * CTILES:(c + 1) * CTILES, :])

        def latents(c):
            t0 = c * CTILES
            tiles = slice(t0, t0 + CTILES)
            part = latn[c % 2]
            done = yield from layer_norm(lat[:, tiles, :], part, CTILES, lat_got[c], latents_ready.get(t0 - 2 * CTILES))
            for t in range(t0, t0 + CTILES):
                norm_sq = act.do(lambda e: e.activation(lat[:, t, :], part[:, t - t0, :], ACT.Square,
                                                        accum_out=bb[:, t:t + 1]), done)
            for t in range(t0, t0 + CTILES, 2):
                turned = transpose_pair(part, t - t0, latT[:, :, t * P:(t + 2) * P], -2.0, 6 + t // 2 % 2, done)
                latents_ready[t] = latents_ready[t + 1] = turned
            for t in range(t0, t0 + CTILES):
                latents_ready[t] = turned
            yield

        ctxT_in = [Slot(sem(f"ctxT_in{i}")) for i in range(4)]
        ctxT_free, ctxT_got = [[], [], [], []], {}
        LOADS = 2 * TILES
        ctxT_of = lambda n: n % 4 if n < LOADS // GROUPS else n % 2
        dist_out = [Slot(sem(f"dist_out{i}")) for i in range(2)]
        dist_sent = [None, None]
        sq_free, unit_free = [None, None], [None, None]
        table_ready, scratch_free = {}, {}

        def load_ctxT(n):
            i = ctxT_of(n)
            pair, half = divmod(n, 2)
            c0, c1 = half * HC, min(N, (half + 1) * HC)
            for b in range(2):
                ctxT_got[n] = ctxT_in[i].dma(
                    sp, ctxT[i][:, b, :, 0:c1 - c0],
                    ctx_tr[2 * pair + b].rearrange("(k p) i -> p k i", p=P)[:, :, c0:c1], *ctxT_free[i])

        def clear_table(g, *ready):
            tb = table[g]
            pool.do(lambda e: e.memset(tb[:, 0:SEGS, :], BIG), *ready)
            pool.do(lambda e: e.memset(tb[:, T + 1:SLOTS, :], BIG))
            pool.do(lambda e: e.memset(tb[:, SEGS:T + 1, 1 + N - (SEGS - 1) * L:W], BIG))
            return pool.do(lambda e: e.memset(tb[:, SEGS:T + 1, 0:1], BIG))

        def unit_rows(u):
            return min(N, (u % QUARTERS + 1) * QC) - u % QUARTERS * QC

        def squares(u):
            n, q = divmod(u, 2)
            nq, i = unit_rows(u), u % 2
            return act.do(lambda e: e.activation(sq[i][:, :, :, 0:nq], ctxT[ctxT_of(n)][:, :, :, q * QC:q * QC + nq], ACT.Square),
                          ctxT_got[n], sq_free[i])

        def distance_products(u, squared):
            n, half = divmod(u, 2)
            pair, q = divmod(u, QUARTERS)
            nq, i, bank = unit_rows(u), u % 2, u % 3
            ps = psum[bank]
            pe.wait(ctxT_got[n], bank_free[bank], latents_ready[pair], c_ones)
            for k in range(KC):
                for b in range(2):
                    read_ctxT = pe.do(lambda e: e.matmul(
                        ps[b * T:(b + 1) * T, 0:nq], latT[:, k, pair * P + b * T:pair * P + (b + 1) * T],
                        ctxT[ctxT_of(n)][:, b, k, half * QC:half * QC + nq], start=(k == 0), stop=False))
            for k in range(KC):
                for b in range(2):
                    tick = pe.do(lambda e: e.matmul(ps[b * T:(b + 1) * T, 0:nq], ones[:, 0:T], sq[i][:, b, k, 0:nq],
                                                    start=False, stop=(k == KC - 1)), squared)
            sq_free[i] = tick
            if half:
                ctxT_free[ctxT_of(n)] = [read_ctxT, squared]
                following = [m for m in range(n + 1, LOADS) if ctxT_of(m) == ctxT_of(n)]
                if following:
                    load_ctxT(following[0])
            return tick

        def distance_roots(u, product, dve_busy):
            pair, i, nq, bank = u // QUARTERS, u % 2, unit_rows(u), u % 3
            zi, ri = z[i][:, 0:nq], root[i][:, 0:nq]
            if dve_busy:
                z_done = act.do(lambda e: e.activation(zi, psum[bank][:, 0:nq], ACT.Relu, bias=bb[:, pair:pair + 1]),
                                product, unit_free[i])
            else:
                z_done = dve.do(lambda e: e.tensor_scalar(zi, psum[bank][:, 0:nq], bb[:, pair:pair + 1], 0.0, ALU.add,
                                                          ALU.max), product, unit_free[i])
            bank_free[bank] = z_done
            root_done = act.do(lambda e: e.activation(ri, zi, ACT.Sqrt, bias=tiny[:, 0:1]), z_done, unit_free[i], c_tiny)
            sq_done = act.do(lambda e: e.activation(root2[i][:, 0:nq], ri, ACT.Square), root_done)
            return sq_done

        def distance_finish(u, rooted, cleared, dve_busy):
            pair, q = divmod(u, QUARTERS)
            i, nq = u % 2, unit_rows(u)
            zi, ri, di = z[i][:, 0:nq], root[i][:, 0:nq], dist[i][:, 0:nq]
            r2 = root2[i][:, 0:nq]
            err = dve.do(lambda e: e.tensor_tensor(zi, zi, r2, ALU.subtract), rooted)
            slope = dve.do(lambda e: e.tensor_scalar(r2.bitcast(I32), r2.bitcast(I32), -0.5, HALF_RSQRT_MAGIC,
                                                     ALU.mult, ALU.add), err)
            corr = dve.do(lambda e: e.tensor_tensor(zi, zi, r2, ALU.mult), slope)
            done = (pool if dve_busy else dve).do(lambda e: e.tensor_tensor(di, ri, zi, ALU.add), corr, dist_sent[i])
            unit_free[i] = done
            g = pair * 2 // GB
            for s in range(2):
                m = min(L, nq - s * L)
                sg = 2 * q + s
                part = 2 * pair % GB * SEGS + sg
                dist_sent[i] = dist_out[i].dma(
                    sp, table[g][part:part + SEGS + 1:SEGS, 1 + sg:1 + sg + T, 1:1 + m],
                    dist[i][:, s * L:s * L + m], done, cleared)

        def distances(g, cleared, dve_busy):
            per = QUARTERS * TILES // GROUPS
            units = range(g * per, (g + 1) * per)
            squared = squares(units[0])
            rooted = None
            for u in units:
                ready = u + 1 in units and (u + 1) // 2 in ctxT_got
                ahead = squares(u + 1) if ready else None
                product = distance_products(u, squared)
                rooting = distance_roots(u, product, dve_busy)
                if rooted:
                    distance_finish(u - 1, rooted, cleared, dve_busy)
                rooted = rooting
                if u + 1 in units:
                    squared = ahead or squares(u + 1)
                yield
            distance_finish(u, rooted, cleared, dve_busy)
            table_ready[g] = list(dist_sent)
            scratch_free[g] = [*everyone(), *dist_sent]

        down = [31] + list(range(31))
        upwards = list(range(1, 32)) + [0]
        shift_free, code_free, min_free = [None], [None, None], [None, None]
        path_ready = {}

        def align(g):
            tb = table[g]
            dve.wait(*table_ready[g], c_first, c_start, c_row1, c_inject, c_nlast)
            pool.wait(*table_ready[g], c_row75)

            def codes(k0, n, ready):
                mins = col_min[k0 // CB % 2][:, 0:n, :]
                left, diag, up = tb[:, k0:k0 + n, 1:W], tb[:, k0:k0 + n, 0:L], tb[:, k0 + 1:k0 + n + 1, 0:L]
                i = k0 // CB % 2
                a, c = above[i][:, 0:n, :], across[i][:, 0:n, :]
                side = pool.do(lambda e: e.tensor_tensor(c, left, diag, ALU.subtract), *ready, code_free[i])
                gain = pool.do(lambda e: e.tensor_tensor(a, up, mins, ALU.subtract))
                min_free[i] = gain
                yield
                sign = act.do(lambda e: e.activation(c, c, ACT.Sign, bias=tiny[:, 0:1]), side, c_tiny)
                half = act.do(lambda e: e.activation(c, c, ACT.Copy, scale=-0.25), sign)
                yield
                yield
                tied = dve.do(lambda e: e.scalar_tensor_tensor(a, c, TIE, a, ALU.mult, ALU.add), half, gain)
                rc = pool.do(lambda e: e.tensor_tensor(c, bc(row75[:, :], n, 1), c, ALU.add), tied)
                yield
                yield
                code_free[i] = dve.do(lambda e: e.scalar_tensor_tensor(left, a, 0.0, c, ALU.is_gt, ALU.mult), rc)

            halo = scan_done = None
            under_way = []
            for step in range(STEPS):
                prev, cur = tb[:, step, :], tb[:, step + 1, :]
                cm = col_min[step // CB % 2][:, step % CB, :]
                if step:
                    sh = dve.do(lambda e: e.stream_shuffle(shifted[:, 0:1], prev[:, L:W], down), scan_done, shift_free[0])
                m = dve.do(lambda e: e.tensor_tensor(cm, prev[:, 1:W], prev[:, 0:L], ALU.min), halo, scan_done,
                           min_free[step // CB % 2])
                for moves in under_way:
                    next(moves, None)
                if step:
                    halo = shift_free[0] = dve.do(lambda e: e.tensor_scalar(cur[:, 0:1], shifted[:, 0:1],
                                                                            first_big[:, 0:1], None, ALU.max), sh)
                first = start[:, 0:1] if step == 0 else cur[:, 0:1]
                scan_done = dve.do(lambda e: e.tensor_tensor_scan(cur[:, 1:W], cm, cur[:, 1:W], first, ALU.min, ALU.add), m, halo)
                if step % CB == CB - 1 or step == STEPS - 1:
                    k0 = step // CB * CB
                    under_way = under_way[-1:] + [codes(k0, step + 1 - k0, [scan_done, halo])]
                    next(under_way[-1])
                yield
            run(under_way[0])
            run(under_way[1])
            th, best = threshold[g], above[0][:, 0, :]
            t_old = dve.do(lambda e: e.memset(th[:, STEPS:SLOTS], float(N)), *code_free)
            for step in range(STEPS - 1, -1, -1):
                code, old, new = tb[:, step, 1:W], th[:, step + 1:step + 2], th[:, step:step + 1]
                a = dve.do(lambda e: e.scalar_tensor_tensor(best, row1[:, :], old, code, ALU.is_le, ALU.mult), t_old)
                s = dve.do(lambda e: e.stream_shuffle(shifted[:, 0:1], old, upwards), shift_free[0], t_old)
                r = dve.do(lambda e: e.tensor_reduce(reach[:, 0:1], best, AX.X, ALU.max), a)
                t_old = dve.do(lambda e: e.scalar_tensor_tensor(new, shifted[:, 0:1], not_last[:, 0:1], reach[:, 0:1],
                                                                ALU.mult, ALU.max), s, r)
                shift_free[0] = t_old
                if step >= T:
                    t_old = dve.do(lambda e: e.tensor_tensor(new, new, inject[:, step:step + 1], ALU.max), t_old)
                yield
            path_ready[g] = t_old

        load_latents()
        for n in range(4):
            load_ctxT(n)
        run(latents(0))
        cleared0 = clear_table(0)
        interleave(distances(0, cleared0, False), (step for c in range(1, CHUNKS) for step in latents(c)), lambda n: 1)
        cleared1 = clear_table(1, *everyone())
        interleave(distances(1, cleared1, True), align(0), lambda n: CB)
        distances_done = scratch_free[1]
        table0_done = Tick(dve.sem, dve.count)

        x_in = Slot(sem("x_in"))
        got_x = x_in.dma(sp, xr[:, :, :], x_tiles, *distances_done)
        rows_in = [Slot(sem(f"rows_in{i}")) for i in range(ROWS_RING)]
        rows_free, rows_got = [table0_done] * ROWS_RING, {}
        path_free, ends_free, cuts_free = [table0_done] * 3, [table0_done], [table0_done] * 2
        added, cut, masked = {}, {}, {}

        def load_rows(n):
            if n >= 2 * B:
                return
            pair, half, b = n // 4, n // 2 % 2, n % 2
            i, t0 = n % ROWS_RING, half * CTH
            r0, r1 = t0 * P, min(N, (t0 + CTH) * P)
            full = (r1 - r0) // P
            source = ctx_nat[2 * pair + b]
            rows_got[n] = rows_in[i].dma(sp, rows_c[i][:, 0:full, :],
                                         source[r0:r0 + full * P, :].rearrange("(t p) d -> p t d", p=P), rows_free[i])
            if r0 + full * P < r1:
                rows_got[n] = rows_in[i].dma(sp, rows_c[i][0:r1 - r0 - full * P, full, :], source[r0 + full * P:r1, :])

        def path_cut(b):
            if b >= B or b // GB not in path_ready or b in cut:
                return
            g, i, row = b // GB, b % 2, b % GB * SEGS
            tick = pe.do(lambda e: e.matmul(psum[2][:, 0:T + 1], ident[:, row:row + 1].to_broadcast([P, P]),
                                            threshold[g][:, 0:T + 1], start=True, stop=True), bank_free[2], path_ready[g])
            bank_free[2] = cut[b] = act.do(lambda e: e.activation(cuts[i][:, :], psum[2][:, 0:T + 1], ACT.Copy), tick,
                                           cuts_free[i])

        def path_mask(b):
            path_cut(b)
            if b in masked or b not in cut:
                return
            i, m = b % 2, b % 3
            rp, lo, hi = bc(rowP[:, :], T, 2), bc(cuts[i][:, 0:T], CT, 1), bc(cuts[i][:, 1:T + 1], CT, 1)
            dve.do(lambda e: e.tensor_tensor(from_row[:, :, :], rp, lo, ALU.is_ge), cut[b], ends_free[0], c_rowP)
            h = dve.do(lambda e: e.tensor_tensor(to_row[:, :, :], rp, hi, ALU.is_le))
            cuts_free[i] = h
            masked[b] = ends_free[0] = pool.do(lambda e: e.tensor_tensor(
                on_path[m][:, :, :], from_row[:, :, :], to_row[:, :, :], ALU.mult), h, path_free[m])

        def add_rows(pairs):
            for pair in pairs:
                for b in range(3):
                    path_mask(2 * pair + b)
                yield
                bank = pair % 2
                pe.wait(bank_free[bank], masked[2 * pair], masked[2 * pair + 1])
                for half in range(2):
                    loads = [4 * pair + 2 * half + b for b in range(2)]
                    pe.wait(*(rows_got[n] for n in loads))
                    for t in range(half * CTH, min(CT, (half + 1) * CTH)):
                        k = min(P, N - t * P)
                        for b in range(2):
                            tick = pe.do(lambda e: e.matmul(
                                psum[bank][b * T:(b + 1) * T, 0:D], on_path[(2 * pair + b) % 3][0:k, t, :],
                                rows_c[loads[b] % ROWS_RING][0:k, t - half * CTH, :], start=(t == 0), stop=(t == CT - 1)))
                    for n in loads:
                        rows_free[n % ROWS_RING] = tick
                    for n in loads:
                        load_rows(n + ROWS_RING)
                    yield
                for b in range(2):
                    path_free[(2 * pair + b) % 3] = tick
                    path_cut(2 * pair + 3 + b)
                yield
                bank_free[bank] = added[pair] = dve.do(lambda e: e.tensor_tensor(
                    xr[:, pair, :], xr[:, pair, :], psum[bank][:, 0:D], ALU.add), tick, got_x)
                yield

        rec_in = Slot(sem("rec_in"))

        def load_recurrence():
            for tile_, source in ((w_k, wk), (w_r, wr_t), (w_v, wv_t), (w_w, ww_t), (w_o, wo_t), (w_g, gate_t)):
                got = rec_in.dma(sp, tile_[:, :, :], source.rearrange("(k p) n -> p k n", p=P), *distances_done)
            return got

        def key_weights(got):
            for k in range(KC):
                pe.wait(got, c_blocks, bank_free[3 + k])
                for oc in range(KC):
                    tick = pe.do(lambda e: e.matmul(psum[3 + k][:, oc * P:(oc + 1) * P], w_k[:, oc, k * P:(k + 1) * P],
                                                    blocks[:, :], start=True, stop=True))
                bank_free[3 + k] = act.do(lambda e: e.activation(w_ks[:, k, :], psum[3 + k][:, 0:D], ACT.Copy), tick, got)
            return bank_free[3 + KC - 1]

        latents2_out = Slot(sem("latents2_out"))
        chunk_end = {-1: []}
        h2T_ready, h2T_free = {}, [None, None]
        stored = [None]

        def recurrence(c):
            t0 = c * CTILES
            free = chunk_end[c - 1]
            y_done = yield from layer_norm(xr[:, t0:t0 + CTILES, :], hn, CTILES, *(added[t] for t in range(t0, t0 + CTILES)),
                                *free, stored[0], *distances_done)
            yield
            for t in range(0, CTILES, 2):
                hT_done = transpose_pair(hn, t, hT[:, :, t * P:(t + 2) * P], 1.0, 3 + t // 2, y_done, *free)
            yield

            def project(w, oc, bank):
                pe.wait(bank_free[bank], hT_done, *recurrence_ready)
                for k in range(KC):
                    tick = pe.do(lambda e: e.matmul(psum[bank][:, :], w[:, k, oc * P:(oc + 1) * P], hT[:, k, :],
                                                    start=(k == 0), stop=(k == KC - 1)))
                return tick

            s_done = m_done = None
            for oc in range(KC):
                p = project(w_r, oc, 3)
                r_done = bank_free[3] = act.do(lambda e: e.activation(gate_r[:, :], psum[3][:, :], ACT.Sigmoid), p,
                                              m_done)
                p = project(w_w, oc, 4)
                w_done = bank_free[4] = act.do(lambda e: e.activation(decay[:, :], psum[4][:, :], ACT.Sigmoid), p,
                                              s_done)
                yield
                p = project(w_v, oc, 5)
                v_done = bank_free[5] = act.do(lambda e: e.activation(val[:, oc, :], psum[5][:, :], ACT.Copy), p)
                p = project(w_ks, oc, 2)
                w_done = dve.do(lambda e: e.tensor_scalar(decay[:, :], decay[:, :], 0.99, None, ALU.mult), w_done)
                w_done = dve.do(lambda e: e.memset(decay[:, 0:CH:T], 0.0), w_done)
                kv_done = bank_free[2] = dve.do(lambda e: e.tensor_tensor(kv[:, oc, :], psum[2][:, :], val[:, oc, :],
                                                                          ALU.mult), p, v_done)
                yield
                s_done = dve.do(lambda e: e.tensor_tensor_scan(kv[:, oc, :], decay[:, :], kv[:, oc, :], 0.0,
                                                               ALU.mult, ALU.add), w_done, kv_done)
                m_done = dve.do(lambda e: e.tensor_tensor(mix[:, oc, :], gate_r[:, :], kv[:, oc, :], ALU.mult),
                                s_done, r_done)
                m2_done = act.do(lambda e: e.activation(mix2[:, oc, :], mix[:, oc, :], ACT.Square), m_done, kv_done)
                yield
            pe.wait(m2_done, bank_free[2])
            for t in range(CTILES):
                for k in range(KC):
                    tick = pe.do(lambda e: e.matmul(psum[2][:, t:t + 1], mix2[:, k, t * P:(t + 1) * P], ones[:, 0:1],
                                                    start=(k == 0), stop=(k == KC - 1)))
            squares_read = tick
            r1 = bank_free[2] = dve.do(lambda e: e.tensor_scalar(rms[:, :], psum[2][:, 0:CTILES], 1.0 / D, EPS_RMS,
                                                                 ALU.mult, ALU.add), tick)
            r2 = act.do(lambda e: e.activation(rms2[:, :], rms[:, :], ACT.Sqrt), r1)
            r3 = dve.do(lambda e: e.reciprocal(rms[:, :], rms2[:, :]), r2)
            yield
            for t in range(CTILES):
                bank = 4 + t % 2
                pe.wait(bank_free[bank], m_done)
                for k in range(KC):
                    tick = pe.do(lambda e: e.matmul(psum[bank][:, 0:D], mix[:, k, t * P:(t + 1) * P], w_o[:, k, :],
                                                    start=(k == 0), stop=(k == KC - 1)))
                x_done = bank_free[bank] = dve.do(lambda e: e.scalar_tensor_tensor(
                    xr[:, t0 + t, :], psum[bank][:, 0:D], rms[:, t:t + 1], xr[:, t0 + t, :], ALU.mult, ALU.add), tick, r3)
            mix_read = tick
            yield
            y_done = yield from layer_norm(xr[:, t0:t0 + CTILES, :], hn, CTILES, x_done, squares_read)
            stored[0] = latents2_out.dma(sp, latents2.rearrange("(n p) d -> p n d", p=P)[:, t0:t0 + CTILES, :], hn[:, :, :],
                                         y_done)
            yield
            hb = h2T[c % 2]
            for t in range(0, CTILES, 2):
                h2_done = transpose_pair(hn, t, hb[:, :, t * P:(t + 2) * P], 1.0, 3 + t // 2, y_done, h2T_free[c % 2])
            h2T_ready[c] = h2_done
            pe.wait(h2_done, bank_free[2])
            for t in range(CTILES):
                for k in range(KC):
                    tick = pe.do(lambda e: e.matmul(psum[2][:, t * E:(t + 1) * E], hb[:, k, t * P:(t + 1) * P], w_g[:, k, :],
                                                    start=(k == 0), stop=(k == KC - 1)))
            yield
            g0 = bank_free[2] = dve.do(lambda e: e.tensor_copy(lg[:, :, :], psum[2][:, 0:CTILES * E].rearrange(
                "p (t e) -> p t e", e=E)), tick)
            g1 = dve.do(lambda e: e.tensor_reduce(ssum[:, :], lg[:, :, :], AX.X, ALU.max), g0)
            g2 = dve.do(lambda e: e.tensor_tensor(lg[:, :, :], lg[:, :, :], bc(ssum[:, :], E, 2), ALU.subtract), g1)
            g3 = act.do(lambda e: e.activation(sc[:, :, :], lg[:, :, :], ACT.Exp), g2)
            g4 = dve.do(lambda e: e.tensor_reduce(ssum[:, :], sc[:, :, :], AX.X, ALU.add), g3)
            g5 = dve.do(lambda e: e.reciprocal(ssum[:, :], ssum[:, :]), g4)
            g6 = dve.do(lambda e: e.tensor_tensor(sc[:, :, :], sc[:, :, :], bc(ssum[:, :], E, 2), ALU.mult), g5)
            yield
            for t in range(CTILES):
                g7 = dve.do(lambda e: e.max(top8[:, t, :], sc[:, t, :]), g6)
            for t in range(CTILES):
                g8 = dve.do(lambda e: e.max_index(idx[:, t, :], top8[:, t, :], sc[:, t, :]), g7)
            g9 = dve.do(lambda e: e.tensor_copy(idxf[:, :, :], idx[:, :, 0:2]), g8)
            g10 = dve.do(lambda e: e.scalar_tensor_tensor(den[:, :], top8[:, :, 0], 1e-20, top8[:, :, 1], ALU.add, ALU.add), g7)
            g11 = dve.do(lambda e: e.reciprocal(den[:, :], den[:, :]), g10)
            dve.do(lambda e: e.tensor_tensor(weight[:, t0:t0 + CTILES, :], top8[:, :, 0:2], bc(den[:, :], 2, 2), ALU.mult), g11)
            for k in range(2):
                gate_done = dve.do(lambda e: e.tensor_tensor(
                    chosen[:, k, t0:t0 + CTILES, :], bc(expert_io[:, :], CTILES, 1),
                    idxf[:, :, k:k + 1].to_broadcast([P, CTILES, E]), ALU.is_equal), g9, c_expert)
            chunk_end[c] = [mix_read, squares_read, gate_done, h2_done]
            yield

        src_in = [Slot(sem(f"src_in{i}")) for i in range(3)]
        y_out = [Slot(sem(f"y_out{i}")) for i in range(2)]
        src_free, srcT_free, y_sent = [None] * 3, [None, None], [None, None]
        act_free, hid_free, hidT_free = [None, None], [None, None], [None, None]
        loaded = {}
        shared_done = {}
        routed_ready = []

        def load_source(k):
            if k < MOE_TILES:
                slot = src_in[k % 3]
                slot.count += 16
                pool.wait(*routed_ready, src_free[k % 3])
                pool.engine.indirect_dma_start(
                    out=src[k % 3][:, :], out_offset=None, in_=latents2[:, :],
                    in_offset=bass.IndirectOffsetOnAxis(ap=order[:, k:k + 1], axis=0)).then_inc(slot.sem, 16)
                loaded[k] = Tick(slot.sem, slot.count)

        def experts(units):
            state = {}

            def prepare(j):
                kind, t = units[j]
                if kind == "shared":
                    state[j] = dict(x=lambda k: h2T[t // CTILES % 2][:, k, t % CTILES * P:(t % CTILES + 1) * P],
                                    ready=[h2T_ready[t // CTILES], shared_ready],
                                    up=lambda m, k, c0: ws_up[:, m, k, c0:c0 + HH], dn=lambda r, c: ws_dn[0:r, c, :])
                    return
                i = t % 2
                pe.wait(loaded[t], bank_free[5], c_ident)
                for k in range(KC):
                    tick = pe.do(lambda e: e.transpose(psum[5][:, k * P:(k + 1) * P], src[t % 3][:, k * P:(k + 1) * P],
                                                       ident[:, :]))
                src_free[t % 3] = tick
                load_source(t + 3)
                bank_free[5] = act.do(lambda e: e.activation(srcT[i][:, :, :], psum[5][:, 0:D].rearrange(
                    "p (k n) -> p k n", k=KC), ACT.Copy), tick, srcT_free[i])
                pe.wait(known["experts"])
                ex = pe.engine.value_load(tile_expert[0:1, t:t + 1], min_val=0, max_val=E - 1)
                state[j] = dict(x=lambda k: srcT[i][:, k, :], ready=[bank_free[5], *weights_ready],
                                up=lambda m, k, c0: w_up[:, bass.ds(ex, 1), m, k, c0:c0 + HH],
                                dn=lambda r, c: w_dn[0:r, bass.ds(ex, 1), c, :])

            def up(h):
                j, half = divmod(h, 2)
                s, i = state[j], h % 2
                for m in range(2):
                    bank = 2 * i + m
                    pe.wait(bank_free[bank], *s["ready"])
                    for k in range(KC):
                        tick = pe.do(lambda e: e.matmul(psum[bank][:, 0:HH], s["x"](k), s["up"](m, k, half * HH),
                                                        start=(k == 0), stop=(k == KC - 1)))
                    if m == 0:
                        bank_free[bank] = silu = act.do(lambda e: e.activation(act_s[i][:, :], psum[bank][:, 0:HH], ACT.Silu),
                                                        tick, act_free[i])
                if half:
                    if units[j][0] == "shared":
                        h2T_free[units[j][1] // CTILES % 2] = tick
                    else:
                        srcT_free[units[j][1] % 2] = tick
                bank_free[bank] = act_free[i] = s[("hid", half)] = dve.do(lambda e: e.tensor_tensor(
                    hid[i][:, :], psum[bank][:, 0:HH], act_s[i][:, :], ALU.mult), tick, silu, hid_free[i])

            def turn(h):
                j, half = divmod(h, 2)
                s, i = state[j], h % 2
                pe.wait(bank_free[4], s[("hid", half)])
                for c in range(HC3):
                    r = min(P, HH - c * P)
                    tick = pe.do(lambda e: e.transpose(psum[4][0:r, c * P:(c + 1) * P], hid[i][:, c * P:c * P + r], ident[:, :]))
                hid_free[i] = tick
                full = HH // P
                a = act.do(lambda e: e.activation(hidT[i][:, 0:full, :], psum[4][:, 0:full * P].rearrange(
                    "p (c n) -> p c n", c=full), ACT.Copy), tick, hidT_free[i])
                r = HH - full * P
                d = dve.do(lambda e: e.tensor_copy(hidT[i][0:r, full, :], psum[4][0:r, full * P:(full + 1) * P]), tick,
                           hidT_free[i], a)
                bank_free[4] = d
                s[("T", half)] = [a, d]

            def down_(h):
                j, half = divmod(h, 2)
                s, i = state[j], h % 2
                kind, t = units[j]
                bank = 6 + j % 2
                pe.wait(*s[("T", half)])
                if half == 0:
                    pe.wait(bank_free[bank])
                for c in range(HC3):
                    r = min(P, HH - c * P)
                    tick = pe.do(lambda e: e.matmul(psum[bank][:, 0:D], hidT[i][0:r, c, :], s["dn"](r, half * HC3 + c),
                                                    start=(half == 0 and c == 0), stop=(half == 1 and c == HC3 - 1)))
                hidT_free[i] = tick
                if half == 0:
                    return
                if kind == "shared":
                    bank_free[bank] = shared_done[t] = dve.do(lambda e: e.tensor_tensor(
                        xr[:, t, :], xr[:, t, :], psum[bank][:, 0:D], ALU.add), tick, *chunk_end[t // CTILES])
                else:
                    y = t % 2
                    bank_free[bank] = done_ = dve.do(lambda e: e.tensor_copy(y_sb[y][:, :], psum[bank][:, 0:D]), tick,
                                                     y_sent[y], *routed_ready)
                    y_sent[y] = y_out[y].dma(sp, sorted_out[t * P:(t + 1) * P, :], y_sb[y][:, :], done_)
                del state[j]

            n = 2 * len(units)
            prepare(0)
            for h in range(n + 2):
                if h < n:
                    up(h)
                if h % 2 == 0 and h // 2 + 1 < len(units):
                    prepare(h // 2 + 1)
                if 0 <= h - 1 < n:
                    turn(h - 1)
                if 0 <= h - 2 < n:
                    down_(h - 2)
                yield

        def load_weights(slot, up_tile, dn_tile, n, *ready, parts=("up", "dn")):
            if "up" in parts:
                for m, source in enumerate((w1_t, w3_t)):
                    tick = slot.dma(sp, up_tile[:, m, :, :], source[n].rearrange("(k p) n -> p k n", p=P), *ready)
            if "dn" in parts:
                full = HH // P
                for half in range(2):
                    r0 = half * HH
                    slot.dma(sp, dn_tile[:, half * HC3:half * HC3 + full, :],
                             w2_t[n, r0:r0 + full * P, :].rearrange("(k p) n -> p k n", p=P), *ready)
                    tick = slot.dma(sp, dn_tile[0:HH - full * P, half * HC3 + full, :], w2_t[n, r0 + full * P:r0 + HH, :])
            return tick

        recurrence_got = load_recurrence()
        recurrence_ready = []
        shared_ready = load_weights(Slot(sem("shared_in")), ws_up, ws_dn, E, *distances_done)
        for n in range(ROWS_RING):
            load_rows(n)
        shared_tiles = lambda tiles: experts([("shared", t) for t in tiles])

        def behind_first():
            yield from add_rows(range(0, 4))
            recurrence_ready.append(key_weights(recurrence_got))
            yield from together(recurrence(0), add_rows(range(4, 8)))
            yield from together(recurrence(1), shared_tiles(range(0, 4)))
            yield from shared_tiles(range(4, 8))

        interleave(align(1), behind_first(), lambda n: min(n % 4, 1) if n > LEAD else 0)
        table1_done = Tick(dve.sem, dve.count)
        up_in, dn_in = Slot(sem("up_in")), Slot(sem("dn_in"))
        run(add_rows(range(8, 12)))
        run(together(recurrence(2), add_rows(range(12, 16))))
        path_done = everyone()
        for n in range(E):
            dn_got = load_weights(dn_in, None, w_dn[:, n], n, *path_done, parts=("dn",))
        early = (align_end - table_at[1]) // W_UP
        for n in range(early):
            load_weights(up_in, w_up[:, n], None, n, table1_done, parts=("up",))
        run(together(recurrence(3), shared_tiles(range(8, 11))))

        rec_done = [*everyone(), stored[0]]
        for n in range(early, E):
            up_got = load_weights(up_in, w_up[:, n], None, n, *rec_done, parts=("up",))
        counts, totals = psum[5][:, 0:TILES * E], psum[5][:, TILES * E:2 * TILES * E]
        places = psum[5][:, 2 * TILES * E:2 * TILES * E + MOE_TILES]
        known = {}

        def slots():
            c_reset = dve.do(lambda e: e.memset(reset[:, :, :], 1.0), *rec_done)
            c_reset = dve.do(lambda e: e.memset(reset[:, :, 0:1], 0.0), c_reset)
            c_tile = pool.do(lambda e: e.iota(tile_io[:, :], [[1, MOE_TILES]], base=0, channel_multiplier=0,
                                              allow_small_or_imprecise_dtypes=True), *rec_done)
            c_no = pool.do(lambda e: e.iota(tile_no[:, :], [[1, MOE_TILES]], base=0, channel_multiplier=0,
                                            allow_small_or_imprecise_dtypes=True))
            c_no = pool.do(lambda e: e.iota(place_no[:, :], [[1, P]], base=0, channel_multiplier=0,
                                            allow_small_or_imprecise_dtypes=True))
            c_no = pool.do(lambda e: e.iota(token_no[:, :], [[P, TILES]], base=0, channel_multiplier=1,
                                            allow_small_or_imprecise_dtypes=True))
            both = dve.do(lambda e: e.tensor_tensor(prod[:, :, :], chosen[:, 0, :, :], chosen[:, 1, :, :], ALU.add), *rec_done)
            flat = lambda tile_: tile_[:, :, :].rearrange("p t e -> p (t e)")
            pe.wait(bank_free[5], c_before, both)
            pe.do(lambda e: e.matmul(counts, before[:, :], flat(prod), start=True, stop=True))
            s0 = pe.do(lambda e: e.matmul(totals, ones[:, :], flat(prod), start=True, stop=True))
            s1 = dve.do(lambda e: e.tensor_copy(tot_e[:, :, :], totals.rearrange("p (t e) -> p e t", e=E)), s0)
            s2 = dve.do(lambda e: e.tensor_tensor_scan(incl[:, :, :].rearrange("p e t -> p (e t)"),
                                                       reset[:, :, :].rearrange("p e t -> p (e t)"),
                                                       tot_e[:, :, :].rearrange("p e t -> p (e t)"), 0.0, ALU.mult, ALU.add),
                        s1, c_reset)
            yield
            s3 = dve.do(lambda e: e.tensor_scalar(tiles_i[:, :], incl[:, :, TILES - 1], float(P - 1), None, ALU.add), s2)
            s4 = dve.do(lambda e: e.tensor_single_scalar(tiles_i[:, :], tiles_i[:, :], 7, ALU.logical_shift_right), s3)
            s5 = dve.do(lambda e: e.tensor_copy(tiles_f[:, :], tiles_i[:, :]), s4)
            s6 = dve.do(lambda e: e.tensor_tensor_scan(tiles_cum[:, :], ones[:, 0:E], tiles_f[:, :], 0.0, ALU.mult, ALU.add), s5)
            s7 = dve.do(lambda e: e.tensor_tensor(cmp[:, :, :], bc(tile_io[:, :], E, 2), bc(tiles_cum[:, :], MOE_TILES, 1),
                                                  ALU.is_ge), s6, c_tile)
            s8 = dve.do(lambda e: e.tensor_reduce(tile_io[:, :], cmp[:, :, :], AX.X, ALU.add), s7)
            known["experts"] = dve.do(lambda e: e.tensor_scalar(tile_expert[:, :], tile_io[:, :], float(E - 1), None, ALU.min), s8)
            yield
            p0 = dve.do(lambda e: e.tensor_tensor(tiles_f[:, :], tiles_cum[:, :], tiles_f[:, :], ALU.subtract), s6)
            p1 = dve.do(lambda e: e.tensor_tensor(incl[:, :, :], incl[:, :, :], tot_e[:, :, :], ALU.subtract), s3)
            p2 = dve.do(lambda e: e.tensor_tensor(base[:, :, :], counts.rearrange("p (t e) -> p t e", e=E),
                                                  incl[:, :, :].rearrange("p e t -> p t e"), ALU.add), p1)
            p3 = dve.do(lambda e: e.scalar_tensor_tensor(base[:, :, :], bc(tiles_f[:, :], TILES, 1), float(P), base[:, :, :],
                                                         ALU.mult, ALU.add), p0, p2)
            for k in range(2):
                p4 = dve.do(lambda e: e.tensor_tensor(prod[:, :, :], chosen[:, k, :, :], base[:, :, :], ALU.mult), p3, s0)
                p3 = dve.do(lambda e: e.tensor_reduce(slot_f[:, :, k], prod[:, :, :], AX.X, ALU.add), p4)
            slots_known = dve.do(lambda e: e.tensor_copy(slot_i[:, :, :], slot_f[:, :, :]), p3)
            yield
            q0 = dve.do(lambda e: e.tensor_single_scalar(tile_of_i[:, :, :], slot_i[:, :, :].bitcast(I32), 7,
                                                         ALU.logical_shift_right), slots_known)
            q1 = dve.do(lambda e: e.tensor_single_scalar(place_of_i[:, :, :], slot_i[:, :, :].bitcast(I32), P - 1,
                                                         ALU.bitwise_and))
            q2 = dve.do(lambda e: e.tensor_copy(tile_of[:, :, :], tile_of_i[:, :, :]), q0)
            q3 = dve.do(lambda e: e.tensor_copy(place_of[:, :, :], place_of_i[:, :, :]), q1)
            hots_read = [None, None]
            for n in range(2 * CHUNKS):
                k, c, i = n % 2, n // 2, n % 2
                ts = slice(c * CTILES, (c + 1) * CTILES)
                h0 = dve.do(lambda e: e.tensor_tensor(in_tile[i][:, :, :], bc(tile_no[:, :], CTILES, 1),
                                                      tile_of[:, ts, k:k + 1].to_broadcast([P, CTILES, MOE_TILES]),
                                                      ALU.is_equal), q2, c_no, hots_read[i])
                h1 = dve.do(lambda e: e.tensor_tensor(at_place[i][:, :, :], bc(place_no[:, :], CTILES, 1),
                                                      place_of[:, ts, k:k + 1].to_broadcast([P, CTILES, P]),
                                                      ALU.is_equal), q3)
                h2 = dve.do(lambda e: e.tensor_tensor(in_tile[i][:, :, :], in_tile[i][:, :, :],
                                                      bc(token_no[:, ts], MOE_TILES, 2), ALU.mult), h0)
                pe.wait(h1, h2)
                for t in range(CTILES):
                    tick = pe.do(lambda e: e.matmul(places, at_place[i][:, t, :], in_tile[i][:, t, :],
                                                    start=(n == 0 and t == 0), stop=(n == 2 * CHUNKS - 1 and t == CTILES - 1)))
                hots_read[i] = tick
                yield
            order_known = bank_free[5] = dve.do(lambda e: e.tensor_copy(order[:, :], places), tick)
            routed_ready.extend([order_known, slots_known, known["experts"], stored[0]])

        run(together(slots(), shared_tiles(range(11, TILES - LAST))))
        weights_ready = [up_got, dn_got]
        for k in range(3):
            load_source(k)

        run(experts([("routed", k) for k in range(MOE_TILES)]))

        experts_done = [*y_sent, Tick(pe.sem, pe.count)]
        result = Slot(sem("result"))
        out_tiles = out.rearrange("b t d -> (b t) d").rearrange("(n p) d -> p n d", p=P)
        back_in = [Slot(sem(f"back_in{t}")) for t in range(TILES)]
        pool.wait(*experts_done)
        for t in range(TILES):
            for k in range(2):
                back_in[t].count += 16
                pool.engine.indirect_dma_start(
                    out=back[:, t, k, :], out_offset=None, in_=sorted_out[:, :],
                    in_offset=bass.IndirectOffsetOnAxis(ap=slot_i[:, t, k:k + 1], axis=0)).then_inc(back_in[t].sem, 16)

        def add_shares():
            for t in range(TILES):
                done = shared_done[t]
                for k in range(2):
                    done = dve.do(lambda e: e.scalar_tensor_tensor(
                        xr[:, t, :], back[:, t, k, :], weight[:, t, k:k + 1], xr[:, t, :], ALU.mult, ALU.add),
                        Tick(back_in[t].sem, back_in[t].count), done)
                if t % 4 == 3:
                    added_up.append(result.dma(sp, out_tiles[:, t - 3:t + 1, :], xr[:, t - 3:t + 1, :], done))
                yield

        added_up = []
        interleave(shared_tiles(range(TILES - LAST, TILES)), add_shares(), lambda n: 1 if n < 3 else 2)
        sp.wait(added_up[-1])


def kernel(x, ctx_1024, L0_attn_Wr, L0_attn_Wk, L0_attn_Wv, L0_attn_Ww, L0_attn_Wo, L0_ffn_gate_w,
           L0_ffn_w1, L0_ffn_w2, L0_ffn_w3, L0_ffn_sw1, L0_ffn_sw2, L0_ffn_sw3):
    import concourse.bacc as bacc
    from concourse.bass_utils import run_bass_kernel_spmd as run

    experts = lambda w, s: np.concatenate([np.asarray(w), np.asarray(s)[None]], axis=0).transpose(0, 2, 1)
    arrays = dict(
        x=x, ctx_nat=ctx_1024, ctx_tr=np.asarray(ctx_1024).transpose(0, 2, 1),
        wr_t=np.asarray(L0_attn_Wr).T, wk=L0_attn_Wk, wv_t=np.asarray(L0_attn_Wv).T, ww_t=np.asarray(L0_attn_Ww).T,
        wo_t=np.asarray(L0_attn_Wo).T, gate_t=np.asarray(L0_ffn_gate_w).T,
        w1_t=experts(L0_ffn_w1, L0_ffn_sw1), w3_t=experts(L0_ffn_w3, L0_ffn_sw3), w2_t=experts(L0_ffn_w2, L0_ffn_sw2))
    arrays = {f"{n}_dram": np.ascontiguousarray(a) for n, a in arrays.items()}
    nc = bacc.Bacc("TRN2", target_bir_lowering=False, num_devices=1)
    aps = [nc.dram_tensor(n, a.shape, mybir.dt.from_np(a.dtype), kind="ExternalInput").ap() for n, a in arrays.items()]
    result = nc.dram_tensor("out_dram", (B, T, D), F32, kind="ExternalOutput").ap()
    build(nc, *aps, result)
    return run(nc, [arrays], core_ids=[0]).results[0]["out_dram"]
```
